# Optimizing a Trainium2 kernel written in Bass

```python
import numpy as np
import jax
import jax.numpy as jnp

def _softmax(x, axis=-1):
    return jax.nn.softmax(x, axis=axis)
def _gelu(x):
    return jax.nn.gelu(x, approximate=True)
def _silu(x):
    return jax.nn.silu(x)
def _sigmoid(x):
    return jax.nn.sigmoid(x)
def _layernorm(x, axis=-1, eps=1e-5):
    m = jnp.mean(x, axis=axis, keepdims=True)
    v = jnp.var(x, axis=axis, keepdims=True)
    return (x - m) / jnp.sqrt(v + eps)
def _scatter_add(tgt, idx, src, axis=0):
    return tgt.at[idx].add(src)
def _segment_sum(src, seg, n):
    return jax.ops.segment_sum(src, seg, n)

kernel_name = 'mk_metaformer_d1_conv_nchw512_ffcb93'

def setup_inputs(seed: int = 0):
    np.random.seed(seed)
    _w = jnp.asarray
    def _rec_inputs():
        import jax
        import jax.numpy as jnp
        _gk = jax.random.key(seed)
        x = -0.0005207 + 1.001 * jax.random.normal(jax.random.fold_in(_gk, 1), (1, 512, 64, 64), jnp.float32)
        return x
    x = _rec_inputs()
    def _L0_conv_setup():
        import jax, jax.numpy as jnp
        import numpy as np
        import math
        DIM = 512
        HEAD_DIM = 64
        NH = DIM // HEAD_DIM
        KERNEL = 7
        H = 64
        W = 64
        N = 1

        def _apply_rotary(x, theta):
            d = theta.shape[-1]
            x1, x2, x3 = (x[..., :d], x[..., d:2 * d], x[..., 2 * d:])
            cos, sin = (jnp.cos(theta), jnp.sin(theta))
            return jnp.concatenate([x1 * cos - x2 * sin, x2 * cos + x1 * sin, x3], axis=-1)

        def _na2d(q, k, v, kernel, scale):
            n, nh, hh, ww, e = q.shape
            si = jnp.clip(jnp.arange(hh) - kernel // 2, 0, hh - kernel)
            sj = jnp.clip(jnp.arange(ww) - kernel // 2, 0, ww - kernel)
            ri = si[:, None] + jnp.arange(kernel)
            cj = sj[:, None] + jnp.arange(kernel)
            kg = k[:, :, ri[:, None, :, None], cj[None, :, None, :], :]
            vg = v[:, :, ri[:, None, :, None], cj[None, :, None, :], :]
            attn = jnp.einsum('nahwe,nahwkle->nahwkl', q, kg) * scale
            attn = jax.nn.softmax(attn.reshape(n, nh, hh, ww, kernel * kernel), axis=-1)
            vg = vg.reshape(n, nh, hh, ww, kernel * kernel, e)
            return jnp.einsum('nahwp,nahwpe->nahwe', attn, vg)
        key = jax.random.key(seed)
        ks = jax.random.split(key, 8)
        hidden_states = jax.random.normal(ks[0], (N, DIM, H, W), jnp.float32)
        yy = jnp.linspace(-1.0, 1.0, H)
        xx = jnp.linspace(-1.0, 1.0, W)
        pos = jnp.stack(jnp.meshgrid(yy, xx, indexing='ij'), axis=-1).astype(jnp.float32)
        d = HEAD_DIM // 2
        log_min, log_max = (math.log(math.pi), math.log(10.0 * math.pi))
        freqs = np.exp(np.linspace(log_min, log_max, NH * d // 4 + 1)[:-1])
        freqs = jnp.asarray(freqs.reshape(d // 4, NH).T, jnp.float32)
        w_qkv = jax.random.normal(ks[1], (3 * DIM, DIM), jnp.float32) * 0.02
        w_dw = jax.random.normal(ks[2], (3 * DIM, 1, 3, 3), jnp.float32) * 0.1
        b_dw = jax.random.normal(ks[3], (3 * DIM,), jnp.float32) * 0.01
        w_out = jax.random.normal(ks[4], (DIM, DIM), jnp.float32) * 0.02
        b_out = jax.random.normal(ks[5], (DIM,), jnp.float32) * 0.01
        return {'hidden_states': hidden_states, 'pos': pos, 'w_qkv': w_qkv, 'w_dw': w_dw, 'b_dw': b_dw, 'freqs': freqs, 'w_out': w_out, 'b_out': b_out}
    _L0_conv_all = _L0_conv_setup()
    _L0_conv_in = {k: v for k, v in _L0_conv_all.items() if k in ('pos', 'w_qkv', 'w_dw', 'b_dw', 'freqs', 'w_out', 'b_out', )}
    del _L0_conv_all

    def _L0_ffn_setup():
        import jax, jax.numpy as jnp
        import numpy as np
        TOP_K = 6
        CAP_FACTOR = 2.0
        key = jax.random.key(seed)
        ks = jax.random.split(key, 9)
        B, S, D, F, E, SH = (4, 2048, 512, 256, 64, 2)
        return {'x': jax.random.normal(ks[0], (B, S, D), jnp.float32), 'router_w': jax.random.normal(ks[1], (E, D), jnp.float32) * 0.02, 'bias': jnp.zeros((E,), jnp.float32), 'shared_w_gate': jax.random.normal(ks[2], (SH, F, D), jnp.float32) * 0.02, 'shared_w_up': jax.random.normal(ks[3], (SH, F, D), jnp.float32) * 0.02, 'shared_w_down': jax.random.normal(ks[4], (SH, D, F), jnp.float32) * 0.02, 'w_gate': jax.random.normal(ks[5], (E, F, D), jnp.float32) * 0.02, 'w_up': jax.random.normal(ks[6], (E, F, D), jnp.float32) * 0.02, 'w_down': jax.random.normal(ks[7], (E, D, F), jnp.float32) * 0.02}
    _L0_ffn_all = _L0_ffn_setup()
    _L0_ffn_in = {k: v for k, v in _L0_ffn_all.items() if k in ('router_w', 'bias', 'shared_w_gate', 'shared_w_up', 'shared_w_down', 'w_gate', 'w_up', 'w_down', )}
    del _L0_ffn_all

    return {
        "x": x,
        "L0_conv_pos": _L0_conv_in["pos"],
        "L0_conv_w_qkv": _L0_conv_in["w_qkv"],
        "L0_conv_w_dw": _L0_conv_in["w_dw"],
        "L0_conv_b_dw": _L0_conv_in["b_dw"],
        "L0_conv_freqs": _L0_conv_in["freqs"],
        "L0_conv_w_out": _L0_conv_in["w_out"],
        "L0_conv_b_out": _L0_conv_in["b_out"],
        "L0_ffn_router_w": _L0_ffn_in["router_w"],
        "L0_ffn_bias": _L0_ffn_in["bias"],
        "L0_ffn_shared_w_gate": _L0_ffn_in["shared_w_gate"],
        "L0_ffn_shared_w_up": _L0_ffn_in["shared_w_up"],
        "L0_ffn_shared_w_down": _L0_ffn_in["shared_w_down"],
        "L0_ffn_w_gate": _L0_ffn_in["w_gate"],
        "L0_ffn_w_up": _L0_ffn_in["w_up"],
        "L0_ffn_w_down": _L0_ffn_in["w_down"],
    }

def reference(x, L0_conv_pos, L0_conv_w_qkv, L0_conv_w_dw, L0_conv_b_dw, L0_conv_freqs, L0_conv_w_out, L0_conv_b_out, L0_ffn_router_w, L0_ffn_bias, L0_ffn_shared_w_gate, L0_ffn_shared_w_up, L0_ffn_shared_w_down, L0_ffn_w_gate, L0_ffn_w_up, L0_ffn_w_down):
    import jax
    import jax.numpy as jnp
    def _L0_conv_ref(hidden_states, pos, w_qkv, w_dw, b_dw, freqs, w_out, b_out):
        import jax, jax.numpy as jnp
        import numpy as np
        import math
        DIM = 512
        HEAD_DIM = 64
        NH = DIM // HEAD_DIM
        KERNEL = 7
        H = 64
        W = 64
        N = 1

        def _apply_rotary(x, theta):
            d = theta.shape[-1]
            x1, x2, x3 = (x[..., :d], x[..., d:2 * d], x[..., 2 * d:])
            cos, sin = (jnp.cos(theta), jnp.sin(theta))
            return jnp.concatenate([x1 * cos - x2 * sin, x2 * cos + x1 * sin, x3], axis=-1)

        def _na2d(q, k, v, kernel, scale):
            n, nh, hh, ww, e = q.shape
            si = jnp.clip(jnp.arange(hh) - kernel // 2, 0, hh - kernel)
            sj = jnp.clip(jnp.arange(ww) - kernel // 2, 0, ww - kernel)
            ri = si[:, None] + jnp.arange(kernel)
            cj = sj[:, None] + jnp.arange(kernel)
            kg = k[:, :, ri[:, None, :, None], cj[None, :, None, :], :]
            vg = v[:, :, ri[:, None, :, None], cj[None, :, None, :], :]
            attn = jnp.einsum('nahwe,nahwkle->nahwkl', q, kg) * scale
            attn = jax.nn.softmax(attn.reshape(n, nh, hh, ww, kernel * kernel), axis=-1)
            vg = vg.reshape(n, nh, hh, ww, kernel * kernel, e)
            return jnp.einsum('nahwp,nahwpe->nahwe', attn, vg)
        scale = HEAD_DIM ** (-0.5)
        qkv = jnp.einsum('nchw,oc->nohw', hidden_states, w_qkv)
        qkv = jax.lax.conv_general_dilated(qkv, w_dw, (1, 1), 'SAME', dimension_numbers=('NCHW', 'OIHW', 'NCHW'), feature_group_count=qkv.shape[1]) + b_dw[None, :, None, None]
        n, c3, hh, ww = qkv.shape
        q, k, v = [t.reshape(n, NH, HEAD_DIM, hh, ww).transpose(0, 1, 3, 4, 2) for t in jnp.split(qkv, 3, axis=1)]
        theta_h = pos[..., None, 0:1] * freqs
        theta_w = pos[..., None, 1:2] * freqs
        theta = jnp.concatenate([theta_h, theta_w], axis=-1).transpose(2, 0, 1, 3)
        q = _apply_rotary(q, theta)
        k = _apply_rotary(k, theta)
        out = _na2d(q, k, v, KERNEL, scale)
        out = out.transpose(0, 1, 4, 2, 3).reshape(n, NH * HEAD_DIM, hh, ww)
        out = jnp.einsum('nchw,oc->nohw', out, w_out) + b_out[None, :, None, None]
        return out

    def _L0_ffn_ref(x, router_w, bias, shared_w_gate, shared_w_up, shared_w_down, w_gate, w_up, w_down):
        import jax, jax.numpy as jnp
        import numpy as np
        TOP_K = 6
        CAP_FACTOR = 2.0
        B, S, D = x.shape
        E = router_w.shape[0]
        K = TOP_K
        N = B * S
        C = max(1, int(N * K * CAP_FACTOR / E))
        router_logits = jnp.einsum('bsd,ed->bse', x, router_w) + bias
        hg = jnp.einsum('bsd,efd->bsef', x, shared_w_gate)
        hu = jnp.einsum('bsd,efd->bsef', x, shared_w_up)
        shared_out = jnp.einsum('bsef,edf->bsd', jax.nn.silu(hg) * hu, shared_w_down)
        shared_out = shared_out / shared_w_gate.shape[0]
        router_probs = jax.nn.softmax(router_logits, axis=-1)
        topk_p, topk_i = jax.lax.top_k(router_probs, K)
        topk_p = topk_p / (jnp.sum(topk_p, axis=-1, keepdims=True) + 1e-09)
        x_flat = x.reshape(N, D)
        flat_e = topk_i.reshape(-1)
        flat_g = topk_p.reshape(-1)
        token_ids = jnp.repeat(jnp.arange(N), K)
        order = jnp.argsort(flat_e)
        se = flat_e[order]
        st = token_ids[order]
        sg = flat_g[order]
        M = se.shape[0]
        pos = jnp.arange(M)
        is_first = jnp.concatenate([jnp.ones((1,), bool), se[1:] != se[:-1]])
        group_starts = jax.lax.cummax(pos * is_first.astype(pos.dtype))
        slot = pos - group_starts
        valid = slot < C
        safe_slot = jnp.where(valid, slot, C)
        expert_in = jnp.zeros((E, C + 1, D), x.dtype).at[se, safe_slot].set(x_flat[st])
        expert_gate = jnp.zeros((E, C + 1), x.dtype).at[se, safe_slot].set(sg)
        expert_tok = jnp.full((E, C + 1), N, jnp.int32).at[se, safe_slot].set(st.astype(jnp.int32))
        expert_mask = jnp.zeros((E, C + 1), bool).at[se, safe_slot].set(valid)
        expert_in = expert_in[:, :C]
        expert_gate = expert_gate[:, :C]
        expert_tok = expert_tok[:, :C]
        expert_mask = expert_mask[:, :C]
        hg = jnp.einsum('ecd,efd->ecf', expert_in, w_gate)
        hu = jnp.einsum('ecd,efd->ecf', expert_in, w_up)
        expert_out = jnp.einsum('ecf,edf->ecd', jax.nn.silu(hg) * hu, w_down)
        fm = expert_mask.reshape(-1)
        dst = jnp.where(fm, expert_tok.reshape(-1), N)
        fg = jnp.where(fm, expert_gate.reshape(-1), jnp.zeros((), x.dtype))
        sparse = jax.ops.segment_sum(fg[:, None] * expert_out.reshape(-1, D), dst, num_segments=N + 1)[:N]
        return shared_out + sparse.reshape(B, S, D)

    def _gn(v, G=32, eps=1e-5):
        B_, C_, H_, W_ = v.shape
        g = v.reshape(B_, G, C_ // G, H_, W_)
        m = jnp.mean(g, axis=(2, 3, 4), keepdims=True)
        s = jnp.var(g, axis=(2, 3, 4), keepdims=True)
        return ((g - m) / jnp.sqrt(s + eps)).reshape(v.shape)

    def _ln_c(v, eps=1e-6):
        m = jnp.mean(v, axis=1, keepdims=True)
        s = jnp.var(v, axis=1, keepdims=True)
        return (v - m) / jnp.sqrt(s + eps)

    def _ln_t(v, eps=1e-5):
        m = jnp.mean(v, axis=-1, keepdims=True)
        s = jnp.var(v, axis=-1, keepdims=True)
        return (v - m) / jnp.sqrt(s + eps)

    def _to_tokens(v):
        B_, C_, H_, W_ = v.shape
        return v.reshape(B_, C_, H_ * W_).transpose(0, 2, 1)
    def _from_tokens(t, like):
        B_, C_, H_, W_ = like.shape
        return t.transpose(0, 2, 1).reshape(B_, C_, H_, W_)

    x = x + _L0_conv_ref(_ln_c(x), L0_conv_pos, L0_conv_w_qkv, L0_conv_w_dw, L0_conv_b_dw, L0_conv_freqs, L0_conv_w_out, L0_conv_b_out)
    t = _to_tokens(x)
    t = t + _L0_ffn_ref(_ln_t(t), L0_ffn_router_w, L0_ffn_bias, L0_ffn_shared_w_gate, L0_ffn_shared_w_up, L0_ffn_shared_w_down, L0_ffn_w_gate, L0_ffn_w_up, L0_ffn_w_down)
    x = _from_tokens(t, x)
    return x


_drawn_inputs = setup_inputs


def setup_inputs(seed=0):
    import zlib

    import numpy as np

    out = dict(_drawn_inputs(seed))
    spreads = {'L0_ffn_bias': (0.0, 0.8)}
    factors = {'L0_conv_pos': 8.0,
     'L0_conv_w_qkv': 6.278,
     'L0_conv_w_dw': 6.146,
     'L0_conv_b_dw': 8.0,
     'L0_conv_freqs': 8.0,
     'L0_conv_w_out': 5.557,
     'L0_conv_b_out': 43.904,
     'L0_ffn_router_w': 4.139,
     'L0_ffn_w_gate': 3.996,
     'L0_ffn_w_up': 3.914,
     'L0_ffn_w_down': 3.92,
     'L0_ffn_shared_w_gate': 8.0,
     'L0_ffn_shared_w_up': 8.0,
     'L0_ffn_shared_w_down': 8.0}
    for name, (base, spread) in spreads.items():
        noise = np.random.default_rng([zlib.crc32(name.encode()), seed]).standard_normal(out[name].shape)
        drawn = base * np.exp(spread * noise) if base else spread * noise
        out[name] = jnp.asarray(drawn.astype(out[name].dtype))
    for name, factor in factors.items():
        out[name] = (out[name] * factor).astype(out[name].dtype)
    return out
```

```python
import concourse.bass as bass
from concourse import mybir
from contextlib import ExitStack

fp32 = mybir.dt.float32
i32 = mybir.dt.int32
u32 = mybir.dt.uint32
ALU = mybir.AluOpType
ACT = mybir.ActivationFunctionType
AX = mybir.AxisListType

C = 512
IMG = 64
N = IMG * IMG
P = 128
CC = C // P
CH = 512
NCH = N // CH
NH = 8
HD = C // NH
RH = 16
KW = 7
WROWS = 8
WIN = WROWS * IMG
NT = N // P
TAPS = 9
E = 64
F = 256
FC = F // P
TOPK = 6
CAP = int(N * TOPK * 2.0 / E)
NB = 256
SLOTS = E * CAP + NB * P
FAR = 4.0 * SLOTS
PAD = IMG + 2
SCALE = HD ** -0.5
EPS1, EPS2 = 1e-6, 1e-5
PI = 3.1415925
TWO_PI = 6.283185307179586
PI_A = 6.28125
PI_B = 0.0019350051879882812
PI_C = TWO_PI - PI_A - PI_B
ROUND = 12582912.0

K_ID, K_BEFORE, K_UPTO, K_IOTA, K_P, K_ROT, K_END = 0, 128, 256, 320, 576, 577, 705


def wait(eng, sem, value):
    if isinstance(value, int) and value <= 0:
        return
    eng.wait_ge(sem, value)


def settled(eng, passed):
    eng.sem_inc(passed, 1)


def turns(eng, count, turn):
    turn(0)
    with eng.Fori(1, count) as j:
        turn(j)


class Chain:

    def __init__(self, eng, sem):
        self.eng, self.sem, self.before, self.base, self.n = eng, sem, 0, 0, 0

    def __call__(self, ins, passed=None):
        ins.then_inc(self.sem, 1)
        self.n += 1
        self.eng.wait_ge(self.sem, self.base + self.n)
        if passed is not None:
            settled(self.eng, passed)

    def enter(self, j, steps):
        self.before, self.steps = self.base + self.n, steps
        if not isinstance(j, int):
            self.base, self.n = (j - 1) * steps + self.before, 0

    def leave(self, j, looped):
        assert self.base + self.n == self.before + self.steps if isinstance(j, int) else self.n == self.steps
        if not isinstance(j, int):
            self.base, self.n = self.before + looped * self.steps, 0


def layernorm_and_tables(nc, x, pos, freq, cos_d, sin_d, xn):
    xv = x.rearrange("(c p) n -> p c n", p=P)
    with ExitStack() as ctx:
        sb = lambda n, s, d=fp32: ctx.enter_context(nc.sbuf_tensor(n, s, d))
        sem = lambda n: ctx.enter_context(nc.semaphore("a_" + n))
        xc = [sb(f"xc{s}", [P, CC, CH]) for s in range(2)]
        sq = [sb(f"sq{s}", [P, CC, CH]) for s in range(2)]
        sd = [sb(f"sd{s}", [P, CH]) for s in range(2)]
        nt = [sb(f"nt{s}", [P, CH]) for s in range(2)]
        mean_w = sb("mean_w", [P, P])
        eps = sb("eps1", [P, 1])
        fr = sb("fr", [P, 1])
        th = sb("th", [P, N])
        half = sb("half", [P, N])
        whole = sb("whole", [P, N])
        ps_m = [ctx.enter_context(nc.psum_tensor(f"ps_m{s}", [P, CH], fp32)) for s in range(2)]
        ps_v = [ctx.enter_context(nc.psum_tensor(f"ps_v{s}", [P, CH], fp32)) for s in range(2)]
        x_in = [sem(f"x_in{s}") for s in range(2)]
        pos_in, setup, mean_done, centred, squared = [
            sem(n) for n in ("pos_in", "setup", "mean_done", "centred", "squared")]
        var_done, sd_done, normed, steps, angles, sines, stored = [
            sem(n) for n in ("var_done", "sd_done", "normed", "dve_steps", "angles", "sines", "stored")]

        with nc.Block() as block:
            @block.sync
            def _(sp):
                sp.dma_start(th[:, :], pos).then_inc(pos_in, 16)
                sp.dma_start(fr[:, :], freq).then_inc(pos_in, 16)

                def turn(j):
                    for s in range(2):
                        wait(sp, normed, 2 * j)
                        sp.dma_start(xc[s][:, :, :], xv[:, :, bass.ds(j * (2 * CH) + s * CH, CH)]).then_inc(x_in[s], 16)

                turns(sp, NCH // 2, turn)
                sp.wait_ge(sines, 1)
                sp.dma_start(sin_d, half[:, :]).then_inc(stored, 16)
                sp.wait_ge(sines, 2)
                sp.dma_start(cos_d, th[:, :]).then_inc(stored, 16)
                sp.wait_ge(stored, 32)

            @block.tensor
            def _(pe):
                pe.wait_ge(setup, 2)

                def turn(j):
                    wait(pe, centred, 2 * j)
                    for s in range(2):
                        pe.wait_ge(x_in[s], j * 16 + 16)
                        for c in range(CC):
                            last = nc.tensor.matmul(ps_m[s][:, :], mean_w[:, :], xc[s][:, c, :], start=c == 0, stop=c == CC - 1)
                        last.then_inc(mean_done, 1)
                    wait(pe, normed, 2 * j)
                    for s in range(2):
                        pe.wait_ge(squared, 2 * j + s + 1)
                        for c in range(CC):
                            last = nc.tensor.matmul(ps_v[s][:, :], mean_w[:, :], sq[s][:, c, :], start=c == 0, stop=c == CC - 1)
                        last.then_inc(var_done, 1)

                turns(pe, NCH // 2, turn)

            @block.scalar
            def _(act):
                act.wait_ge(setup, 2)

                def turn(j):
                    wait(act, var_done, 2 * j)
                    for s in range(2):
                        act.wait_ge(centred, 2 * j + s + 1)
                        nc.scalar.activation(sq[s][:, :, :], xc[s][:, :, :], ACT.Square).then_inc(squared, 1)
                    wait(act, normed, 2 * j)
                    for s in range(2):
                        act.wait_ge(var_done, 2 * j + s + 1)
                        nc.scalar.activation(sd[s][:, :], ps_v[s][:, :], ACT.Sqrt, bias=eps[:, :]).then_inc(sd_done, 1)

                turns(act, NCH // 2, turn)
                act.wait_ge(angles, 1)
                nc.scalar.activation(half[:, :], half[:, :], ACT.Sin).then_inc(sines, 1)
                act.wait_ge(angles, 2)
                nc.scalar.activation(th[:, :], th[:, :], ACT.Sin).then_inc(sines, 1)

            @block.vector
            def _(dve):
                link = Chain(dve, steps)
                nc.vector.memset(mean_w[:, :], 1.0 / C).then_inc(setup, 1)
                nc.vector.memset(eps[:, :], EPS1).then_inc(setup, 1)

                def turn(j):
                    link.enter(j, 10)
                    for s in range(2):
                        dve.wait_ge(mean_done, 2 * j + s + 1)
                        for c in range(CC):
                            last = nc.vector.tensor_tensor(xc[s][:, c, :], xc[s][:, c, :], ps_m[s][:, :], ALU.subtract)
                        last.then_inc(centred, 1)
                    for s in range(2):
                        dve.wait_ge(sd_done, 2 * j + s + 1)
                        link(nc.vector.reciprocal(sd[s][:, :], sd[s][:, :]))
                        link(nc.vector.tensor_tensor(nt[s][:, :], sd[s][:, :], sd[s][:, :], ALU.mult))
                        link(nc.vector.scalar_tensor_tensor(nt[s][:, :], ps_v[s][:, :], EPS1, nt[s][:, :], ALU.add, ALU.mult))
                        link(nc.vector.tensor_scalar(nt[s][:, :], nt[s][:, :], -0.5, 1.5, ALU.mult, ALU.add))
                        link(nc.vector.tensor_tensor(sd[s][:, :], sd[s][:, :], nt[s][:, :], ALU.mult))
                        for c in range(CC):
                            last = nc.vector.tensor_tensor(xn[:, c, bass.ds(j * (2 * CH) + s * CH, CH)], xc[s][:, c, :], sd[s][:, :], ALU.mult)
                        last.then_inc(normed, 1)
                    link.leave(j, NCH // 2 - 1)

                turns(dve, NCH // 2, turn)
                dve.wait_ge(pos_in, 32)
                link(nc.vector.tensor_scalar(th[:, :], th[:, :], fr[:, :], None, ALU.mult))
                link(nc.vector.tensor_scalar(whole[:, :], th[:, :], 1.0 / TWO_PI, ROUND, ALU.mult, ALU.add))
                link(nc.vector.tensor_scalar(whole[:, :], whole[:, :], -ROUND, None, ALU.add))
                link(nc.vector.scalar_tensor_tensor(th[:, :], whole[:, :], -PI_A, th[:, :], ALU.mult, ALU.add))
                link(nc.vector.scalar_tensor_tensor(th[:, :], whole[:, :], -PI_B, th[:, :], ALU.mult, ALU.add))
                link(nc.vector.scalar_tensor_tensor(th[:, :], whole[:, :], -PI_C, th[:, :], ALU.mult, ALU.add))
                nc.vector.tensor_scalar(half[:, :], th[:, :], PI, -PI, ALU.min, ALU.max).then_inc(angles, 1)
                link(nc.vector.tensor_scalar(whole[:, :], th[:, :], TWO_PI / 4, -TWO_PI, ALU.is_gt, ALU.mult))
                link(nc.vector.scalar_tensor_tensor(th[:, :], th[:, :], TWO_PI / 4, whole[:, :], ALU.add, ALU.add))
                nc.vector.tensor_scalar(th[:, :], th[:, :], PI, -PI, ALU.min, ALU.max).then_inc(angles, 1)


def qkv_conv_rotary(nc, w_qkv, taps, cos_d, sin_d, qk_d, v_d, xn, k_sb):
    QK, TILES = 2 * CC, 3 * CC
    with ExitStack() as ctx:
        sb = lambda n, s, d=fp32: ctx.enter_context(nc.sbuf_tensor(n, s, d))
        sem = lambda n: ctx.enter_context(nc.semaphore("b_" + n))
        wt = [sb(f"wt{s}", [P, CC, P]) for s in range(2)]
        tp = [sb(f"tp{s}", [P, TAPS + 1]) for s in range(2)]
        raw = [sb(f"raw{s}", [P, PAD, PAD]) for s in range(2)]
        acc = [sb(f"acc{s}", [P, IMG, IMG]) for s in range(2)]
        cs = sb("cs", [P, N])
        sn = sb("sn", [P, N])
        crossed = sb("crossed", [P, N])
        rot = sb("rot", [P, N])
        ps_q = [ctx.enter_context(nc.psum_tensor(f"ps_q{b}", [P, CH], fp32)) for b in range(4)]
        ps_r = [ctx.enter_context(nc.psum_tensor(f"ps_r{b}", [P, CH], fp32)) for b in range(4)]
        w_in = [sem(f"w_in{s}") for s in range(2)]
        cs_in, borders, product_done, raw_done, conv_step, conv_done = [
            sem(n) for n in ("cs_in", "borders", "product_done", "raw_done", "conv_step", "conv_done")]
        partner_done, crossed_done, direct_done, rotated, qk_out = [
            sem(n) for n in ("partner_done", "crossed_done", "direct_done", "rotated", "qk_out")]
        v_turned, v_copied = [sem(n) for n in ("v_turned", "v_copied")]
        v_out = [sem(f"v_out{s}") for s in range(2)]
        flat = [a[:, :, :].rearrange("p r c -> p (r c)") for a in acc]
        rows = CH // IMG

        with nc.Block() as block:
            @block.sync
            def _(sp):
                def load_tile(i, s):
                    wait(sp, product_done, NCH * (i - 1))
                    wait(sp, conv_done, i - 1)
                    i0 = bass.ds(i, 1)
                    sp.dma_start(wt[s][:, :, :], w_qkv[i0, :, :, :].rearrange("a p c o -> (a p) c o")).then_inc(w_in[s], 16)
                    sp.dma_start(tp[s][:, :], taps[i0, :, :].rearrange("a p t -> (a p) t")).then_inc(w_in[s], 16)

                def load_angles(hp):
                    wait(sp, rotated, 2 * hp)
                    for d, t in ((cs, cos_d), (sn, sin_d)):
                        for a in range(2):
                            src = t[bass.ds(hp * (2 * RH) + a * RH, RH), :]
                            for g in range(2):
                                at = a * HD + g * RH
                                sp.dma_start(d[at:at + RH, :], src).then_inc(cs_in, 16)

                load_tile(0, 0)
                load_tile(1, 1)
                sp.wait_ge(borders, 4)

                def turn(hp):
                    load_angles(hp)
                    for s in range(2):
                        i = 2 * hp + s
                        sp.wait_ge(rotated, i + 1)
                        sp.dma_start(qk_d[bass.ds(i, 1), :, :].rearrange("a p n -> (a p) n"), rot[:, :]).then_inc(qk_out, 16)
                        load_tile(i + 2, s)

                turns(sp, CC, turn)
                for g in range(CC):
                    if g < 2:
                        load_tile(QK + 2 + g, g)
                    sp.wait_ge(v_copied, NCH * (g + 1))
                    dst = v_d.rearrange("(t p) c -> p t c", p=P)[:, :, g * P:(g + 1) * P]
                    sp.dma_start(dst, (rot if g % 2 == 0 else crossed)[:, :].rearrange("p (t c) -> p t c", c=P)).then_inc(v_out[g % 2], 16)
                sp.wait_ge(qk_out, 16 * QK)
                for s in range(2):
                    sp.wait_ge(v_out[s], 16 * (CC // 2))

            @block.tensor
            def _(pe):
                def products(i, s, loads):
                    pe.wait_ge(w_in[s], 32 * loads)
                    for n in range(NCH):
                        wait(pe, raw_done, NCH * i + n - 3)
                        for c in range(CC):
                            last = nc.tensor.matmul(ps_q[n % 4][:, :], wt[s][:, c, :], xn[:, c, n * CH:(n + 1) * CH], start=c == 0, stop=c == CC - 1)
                        last.then_inc(product_done, 1)

                def partners(i, s):
                    pe.wait_ge(conv_done, i + 1)
                    for n in range(NCH):
                        wait(pe, crossed_done, NCH * i + max(n - 3, 0))
                        nc.tensor.matmul(ps_r[n % 4][:, :], k_sb[:, K_ROT:K_ROT + P], flat[s][:, n * CH:(n + 1) * CH],
                                         start=True, stop=True).then_inc(partner_done, 1)

                def turn_values(g, s):
                    pe.wait_ge(conv_done, QK + g + 1)
                    if g == 0:
                        pe.wait_ge(crossed_done, NCH * QK)
                    for n in range(NCH):
                        wait(pe, v_copied, NCH * g + n - 3)
                        for b in range(4):
                            at = n * CH + b * P
                            last = nc.tensor.transpose(ps_r[n % 4][:, b * P:(b + 1) * P], flat[s][:, at:at + P], k_sb[:, K_ID:K_ID + P])
                        last.then_inc(v_turned, 1)

                products(0, 0, 1)

                def turn(hp):
                    products(2 * hp + 1, 1, hp + 1)
                    partners(2 * hp, 0)
                    products(2 * hp + 2, 0, hp + 2)
                    partners(2 * hp + 1, 1)

                turns(pe, CC, turn)
                for g in range(CC):
                    if g < CC - 1:
                        i = QK + g + 1
                        products(i, i % 2, i // 2 + 1)
                    turn_values(g, g % 2)

            @block.scalar
            def _(act):
                def copy_raw(i, s):
                    wait(act, conv_done, i - 1)
                    for n in range(NCH):
                        act.wait_ge(product_done, NCH * i + n + 1)
                        nc.scalar.activation(raw[s][:, 1 + n * rows:1 + (n + 1) * rows, 1:1 + IMG],
                                             ps_q[n % 4][:, :].rearrange("p (r c) -> p r c", c=IMG), ACT.Copy).then_inc(raw_done, 1)

                def copy_values(g):
                    wait(act, v_out[g % 2], 16 * (g // 2))
                    if g == 0:
                        act.wait_ge(qk_out, 16 * QK)
                    if g == 1:
                        act.wait_ge(rotated, QK)
                    for n in range(NCH):
                        act.wait_ge(v_turned, NCH * g + n + 1)
                        nc.scalar.activation((rot if g % 2 == 0 else crossed)[:, n * CH:(n + 1) * CH], ps_r[n % 4][:, :], ACT.Copy).then_inc(v_copied, 1)

                act.wait_ge(borders, 4)
                copy_raw(0, 0)

                def turn(hp):
                    copy_raw(2 * hp + 1, 1)
                    copy_raw(2 * hp + 2, 0)

                turns(act, CC, turn)
                for g in range(CC):
                    if g < CC - 1:
                        copy_raw(QK + g + 1, (g + 1) % 2)
                    copy_values(g)

            @block.vector
            def _(dve):
                def convolve(i, s, loads):
                    dve.wait_ge(w_in[s], 32 * loads)
                    dve.wait_ge(raw_done, NCH * (i + 1))
                    mid = TAPS // 2
                    nc.vector.tensor_scalar(acc[s][:, :, :], raw[s][:, 1:1 + IMG, 1:1 + IMG], tp[s][:, mid:mid + 1],
                                            tp[s][:, TAPS:TAPS + 1], ALU.mult, ALU.add).then_inc(conv_step, 1)
                    others = [t for t in range(TAPS) if t != mid]
                    for m, t in enumerate(others):
                        dve.wait_ge(conv_step, (TAPS - 1) * i + m + 1)
                        dy, dx = divmod(t, 3)
                        nc.vector.scalar_tensor_tensor(acc[s][:, :, :], raw[s][:, dy:dy + IMG, dx:dx + IMG], tp[s][:, t:t + 1], acc[s][:, :, :],
                                                       ALU.mult, ALU.add).then_inc(conv_done if t == others[-1] else conv_step, 1)

                def cross(i, hp):
                    dve.wait_ge(cs_in, 128 * (hp + 1))
                    wait(dve, rotated, i)
                    for n in range(NCH):
                        dve.wait_ge(partner_done, NCH * i + n + 1)
                        at = slice(n * CH, (n + 1) * CH)
                        nc.vector.tensor_tensor(crossed[:, at], ps_r[n % 4][:, :], sn[:, at], ALU.mult).then_inc(crossed_done, 1)

                for s in range(2):
                    nc.vector.memset(raw[s][:, :, :], 0.0).then_inc(borders, 1)
                nc.vector.memset(cs[:, :], 1.0).then_inc(borders, 1)
                nc.vector.memset(sn[:, :], 0.0).then_inc(borders, 1)

                def turn(hp):
                    for s in range(2):
                        i = 2 * hp + s
                        convolve(i, s, hp + 1)
                        cross(i, hp)

                turns(dve, CC, turn)
                for g in range(CC):
                    if g == 1:
                        dve.wait_ge(rotated, QK)
                    if g >= 2:
                        dve.wait_ge(v_turned, NCH * (g - 1))
                    convolve(QK + g, g % 2, QK // 2 + g // 2 + 1)

            @block.gpsimd
            def _(pool):
                def turn(hp):
                    pool.wait_ge(cs_in, 128 * (hp + 1))
                    for s in range(2):
                        i = 2 * hp + s
                        pool.wait_ge(conv_done, i + 1)
                        wait(pool, qk_out, 16 * i)
                        nc.gpsimd.tensor_tensor(rot[:, :], flat[s], cs[:, :], ALU.mult).then_inc(direct_done, 1)
                        pool.wait_ge(direct_done, i + 1)
                        pool.wait_ge(crossed_done, NCH * (i + 1))
                        nc.gpsimd.tensor_tensor(rot[:, :], rot[:, :], crossed[:, :], ALU.add).then_inc(rotated, 1)

                turns(pool, CC, turn)


def attention_and_routing(nc, x_tok, masks, w_out, b_out, router_w, router_b, qk_d, v_d, x1_d, tn_d, ids_d,
                          k_sb, gates, experts_of, slots_of, starts, block_expert, block_row):
    qv = qk_d.rearrange("(h t) p n -> t p h n", t=2)
    xt_v, x1_v, tn_v = (a.rearrange("(t p) c -> t p c", p=P) for a in (x_tok, x1_d, tn_d))
    one_tile = lambda a, t: a[bass.ds(t, 1), :, :].rearrange("a p n -> (a p) n")
    KC = WIN // P
    PAIR = 2 * NH
    PAIRS = NT // 2
    AHEAD, BEHIND = 3, 2
    SB = 2
    with ExitStack() as ctx:
        sb = lambda n, s, d=fp32: ctx.enter_context(nc.sbuf_tensor(n, s, d))
        sem = lambda n: ctx.enter_context(nc.semaphore("c_" + n))
        ps = lambda n: ctx.enter_context(nc.psum_tensor(n, [P, CH], fp32))
        q = [sb(f"q{s}", [P, CC, P]) for s in range(2)]
        k = [sb(f"k{s}", [P, CC, WIN]) for s in range(2)]
        v = [sb(f"v{s}", [P, KC, C]) for s in range(2)]
        mask = sb("mask", [P, 3, WIN])
        xt = [sb(f"xt{s}", [P, C]) for s in range(2)]
        score = [sb(f"score{b}", [P, WIN]) for b in range(4)]
        prob = [sb(f"prob{b}", [P, WIN]) for b in range(4)]
        probT = [sb(f"probT{b}", [P, WIN]) for b in range(4)]
        top, ntop = sb("top", [P, 4]), sb("ntop", [P, 4])
        total = [sb(f"total{s}", [P, NH]) for s in range(2)]
        inv = sb("inv", [P, NH])
        ao, aoT = sb("ao", [P, C]), sb("aoT", [P, C])
        x1 = [sb(f"x1{s}", [P, C]) for s in range(2)]
        tn = [sb(f"tn{s}", [P, C]) for s in range(2)]
        tnT = sb("tnT", [P, C])
        stats, moments = sb("stats", [P, 6]), sb("moments", [P, 2])
        var_eps, power, rstd = sb("var_eps", [P, 1]), sb("power", [P, 1]), sb("rstd", [P, 1])
        wo, bo = sb("wo", [P, CC, C]), sb("bo", [1, C])
        rw, rb = sb("rw", [P, CC, E]), sb("rb", [1, E])
        ones = sb("ones", [P, P])
        logit, expo = sb("logit", [P, E]), sb("expo", [P, E])
        big8, index8, index_f = sb("big8", [P, 8]), sb("index8", [P, 8], u32), sb("index_f", [P, TOPK])
        nbig, esum, gsum = sb("nbig", [P, 1]), sb("esum", [P, 1]), sb("gsum", [P, 1])
        chosen, picked = sb("chosen", [P, TOPK, E]), sb("picked", [P, TOPK, E])
        taken, counts, rank = sb("taken", [P, E]), sb("counts", [P, E]), sb("rank", [P, E])
        slot, fits, row, gate6, away = [sb(n, [P, TOPK]) for n in ("slot", "fits", "row", "gate6", "away")]
        row_to = [sb(f"row_to{s}", [P, TOPK], i32) for s in range(2)]
        token_f = sb("token_f", [P, 1])
        token = [sb(f"token{s}", [P, 1], i32) for s in range(2)]
        zeros = sb("zeros", [P, SLOTS // P], i32)
        n_blocks, n_blocksT, ends = sb("n_blocks", [P, E]), sb("n_blocksT", [E, P]), sb("ends", [E, 1])
        ended = sb("ended", [E, NB])
        be_f, br_f = sb("be_f", [1, NB]), sb("br_f", [1, NB])
        ps_s = [ps(f"ps_s{b}") for b in range(SB)]
        ps_t = [ps(f"ps_t{b}") for b in range(2)]
        ps_o = [ps(f"ps_o{b}") for b in range(2)]
        ps_x, ps_r = ps("ps_x"), ps("ps_r")

        tile_in, xt_in, x1_out, tn_out, ids_out = [
            [sem(f"{n}{s}") for s in range(2)] for n in ("tile_in", "xt_in", "x1_out", "tn_out", "ids_out")]
        w_in, setup, zeroed, counts_set = sem("w_in"), sem("setup"), sem("zeroed"), sem("counts_set")
        scored, masked, ntop_done, exp_done, turned, value_done, heads_done = [
            sem(n) for n in ("scored", "masked", "ntop_done", "exp_done", "turned", "value_done", "heads_done")]
        aoT_done, aoT_copied, projected, x1_done, var_done, rstd_done, tn_done, tnT_done, tnT_copied = [
            sem(n) for n in ("aoT_done", "aoT_copied", "projected", "x1_done", "var_done", "rstd_done", "tn_done", "tnT_done", "tnT_copied")]
        logits_done, nbig_done, routed_exp, taken_done, ranked, rows_done, steps = [
            sem(n) for n in ("logits_done", "nbig_done", "routed_exp", "taken_done", "ranked", "rows_done", "dve_steps")]
        turn_copied = [sem(f"turn_copied{b}") for b in range(2)]
        logits_read = sem("logits_read")
        passed, passed_pool = sem("passed"), sem("passed_pool")
        blocks_done, map_step, map_done = sem("blocks_done"), sem("map_step"), sem("map_done")

        with nc.Block() as block:
            @block.sync
            def _(sp):
                def load_tile(t, s, first):
                    wait(sp, value_done, NH * (t - 1))
                    sp.dma_start(q[s][:, :, :], qv[0][:, :, bass.ds(t * P, P)]).then_inc(tile_in[s], 16)
                    sp.dma_start(k[s][:, :, :], qv[1][:, :, bass.ds(first, WIN)]).then_inc(tile_in[s], 16)
                    sp.dma_start(v[s][:, :, :], v_d[bass.ds(first, WIN), :].rearrange("(c p) n -> p c n", p=P)).then_inc(tile_in[s], 16)
                    wait(sp, x1_done, t - 1)
                    sp.dma_start(xt[s][:, :], one_tile(xt_v, t)).then_inc(xt_in[s], 16)

                for d, src in ((mask[:, :, :], masks.rearrange("m p n -> p m n")), (wo[:, :, :], w_out), (bo[:, :], b_out),
                               (rw[:, :, :], router_w), (rb[:, :], router_b)):
                    sp.dma_start(d, src).then_inc(w_in, 16)
                for t in range(2):
                    load_tile(t, t % 2, 0)
                sp.wait_ge(setup, 5)
                sp.dma_start(ids_d.rearrange("(p n) a -> p (n a)", p=P), zeros[:, :]).then_inc(zeroed, 16)
                for t in range(2, 4):
                    load_tile(t, t % 2, t * P - KW // 2 * IMG)
                with sp.Fori(2, PAIRS - 1) as j:
                    for s in range(2):
                        load_tile(2 * j + s, s, j * (2 * P) + (s * P - KW // 2 * IMG))
                for t in range(NT - 2, NT):
                    load_tile(t, t % 2, N - WIN)
                sp.wait_ge(map_done, 1)

            TAIL = 16

            def tiles(eng, body, tail):
                body(0)
                body(1)
                with eng.Fori(2, PAIRS - 2) as j:
                    body(j)
                body(PAIRS - 2)
                body(PAIRS - 1)
                for step in range(TAIL):
                    tail(NT - 1, 1, PAIRS - 1, step)
                    if step + NH < TAIL:
                        tail(NT - 2, 0, PAIRS - 1, step + NH)

            def tail_between(j, i, tail):
                t, step = i // NH - 1, i % NH
                for back, at in ((0, step), (1, step + NH)):
                    tile = t - back
                    if at < TAIL and not (isinstance(j, int) and 2 * j + tile < 0):
                        tail(2 * j + tile, tile % 2, j + tile // 2, at)

            def is_last(j):
                return isinstance(j, int) and j == PAIRS - 1

            @block.tensor
            def _(pe):
                ident = k_sb[:, K_ID:K_ID + P]

                def score_head(j, i):
                    s, h = i // NH % 2, i % NH
                    if h == 0:
                        pe.wait_ge(tile_in[s], 48 * (j + (1 if i < PAIR else 2)))
                    wait(pe, masked, PAIR * j + i - 1)
                    a = h % 2 * HD
                    nc.tensor.matmul(ps_s[h % SB][:, :], q[s][a:a + HD, h // 2, :], k[s][a:a + HD, h // 2, :],
                                     start=True, stop=True).then_inc(scored, 1)

                def turn_head(j, i):
                    pe.wait_ge(exp_done, PAIR * j + i + 1)
                    wait(pe, turn_copied[i % 2], NH * j + i // 2)
                    for c in range(KC):
                        at = slice(c * P, (c + 1) * P)
                        last = nc.tensor.transpose(ps_t[i % 2][:, at], prob[i % 4][:, at], ident)
                    last.then_inc(turned, 1)

                def value_head(j, i):
                    s, h = i // NH % 2, i % NH
                    pe.wait_ge(turn_copied[i % 2], NH * j + i // 2 + 1)
                    if h == 0:
                        wait(pe, heads_done, 2 * j + i // NH)
                    for c in range(KC):
                        last = nc.tensor.matmul(ps_o[h % 2][:, h // 2 * P:(h // 2 + 1) * P], probT[i % 4][:, c * P:(c + 1) * P],
                                                v[s][:, c, h // 2 * P:(h // 2 + 1) * P], start=c == 0, stop=c == KC - 1)
                    last.then_inc(value_done, 1)

                def turn_tile(src, done):
                    for c in range(CC):
                        at = slice(c * P, (c + 1) * P)
                        last = nc.tensor.transpose(ps_x[:, at], src[:, at], ident)
                    last.then_inc(done, 1)

                def tail(t, s, uses, step):
                    if step == 2:
                        pe.wait_ge(heads_done, t + 1)
                        wait(pe, logits_read, t)
                        turn_tile(ao, aoT_done)
                    if step == 3:
                        pe.wait_ge(aoT_copied, t + 1)
                        nc.tensor.matmul(ps_x[:, :], ones[0:1, :], bo[:, :], start=True, stop=False)
                        for c in range(CC):
                            last = nc.tensor.matmul(ps_x[:, :], aoT[:, c * P:(c + 1) * P], wo[:, c, :], start=False, stop=c == CC - 1)
                        last.then_inc(projected, 1)
                    if step == 5:
                        pe.wait_ge(tn_done, t + 1)
                        turn_tile(tn[s], tnT_done)
                    if step == 6:
                        pe.wait_ge(tnT_copied, t + 1)
                        nc.tensor.matmul(ps_x[:, 0:E], ones[0:1, :], rb[:, :], start=True, stop=False)
                        for c in range(CC):
                            last = nc.tensor.matmul(ps_x[:, 0:E], tnT[:, c * P:(c + 1) * P], rw[:, c, :], start=False, stop=c == CC - 1)
                        last.then_inc(logits_done, 1)
                    if step == 11:
                        pe.wait_ge(taken_done, t + 1)
                        wait(pe, rows_done, t)
                        nc.tensor.matmul(ps_r[:, 0:E], k_sb[:, K_BEFORE:K_BEFORE + P], taken[:, :], start=True, stop=True)
                        nc.tensor.matmul(ps_r[:, E:2 * E], ones[:, :], taken[:, :], start=True, stop=True).then_inc(ranked, 1)

                def body(j):
                    for i in range(PAIR):
                        if not (is_last(j) and i + AHEAD >= PAIR):
                            score_head(j, i + AHEAD)
                        turn_head(j, i)
                        if i >= BEHIND or not (isinstance(j, int) and j == 0):
                            value_head(j, i - BEHIND)
                        tail_between(j, i, tail)
                    if is_last(j):
                        for i in range(PAIR - BEHIND, PAIR):
                            value_head(j, i)

                pe.wait_ge(w_in, 80)
                pe.wait_ge(setup, 5)
                for i in range(AHEAD):
                    score_head(0, i)
                tiles(pe, body, tail)
                pe.wait_ge(blocks_done, 1)
                nc.tensor.transpose(ps_x[0:E, 0:P], n_blocks[:, :], ident).then_inc(map_step, 1)
                pe.wait_ge(blocks_done, 2)
                nc.tensor.matmul(ps_x[0:E, P:P + 1], k_sb[0:E, K_UPTO:K_UPTO + E], n_blocksT[:, 0:1], start=True, stop=True).then_inc(map_step, 1)
                nc.tensor.matmul(ps_x[:, 2 * P:2 * P + E], n_blocksT[:, :], k_sb[0:E, K_BEFORE:K_BEFORE + E], start=True, stop=True).then_inc(map_step, 1)
                pe.wait_ge(blocks_done, 3)
                nc.tensor.matmul(ps_o[0][0:1, 0:NB], ones[0:E, 0:1], ended[:, :], start=True, stop=True)
                nc.tensor.matmul(ps_t[0][0:1, 0:NB], n_blocksT[:, 0:1], ended[:, :], start=True, stop=True).then_inc(map_step, 1)

            @block.scalar
            def _(act):
                def exp_head(j, i):
                    s, h = i // NH % 2, i % NH
                    act.wait_ge(ntop_done, PAIR * j + i + 1)
                    wait(act, turned, PAIR * j + i - 3)
                    if h == 0:
                        wait(act, heads_done, 2 * j + i // NH - 1)
                    nc.scalar.activation(prob[i % 4][:, :], score[i % 4][:, :], ACT.Exp, bias=ntop[:, i % 4:i % 4 + 1], scale=SCALE,
                                         accum_out=total[s][:, h:h + 1]).then_inc(exp_done, 1)

                def tail(t, s, uses, step):
                    if step == 3:
                        act.wait_ge(aoT_done, t + 1)
                        nc.scalar.activation(aoT[:, :], ps_x[:, :], ACT.Copy).then_inc(aoT_copied, 1)
                    if step == 5:
                        act.wait_ge(x1_done, t + 1)
                        act.dma_start(one_tile(x1_v, t), x1[s][:, :]).then_inc(x1_out[s], 16)
                    if step == 6:
                        act.wait_ge(tn_done, t + 1)
                        act.dma_start(one_tile(tn_v, t), tn[s][:, :]).then_inc(tn_out[s], 16)
                    if step == 6:
                        act.wait_ge(tnT_done, t + 1)
                        nc.scalar.activation(tnT[:, :], ps_x[:, :], ACT.Copy).then_inc(tnT_copied, 1)
                    if step == 8:
                        act.wait_ge(nbig_done, t + 1)
                        nc.scalar.activation(expo[:, :], logit[:, :], ACT.Exp, bias=nbig[:, :], accum_out=esum[:, :]).then_inc(routed_exp, 1)

                def body(j):
                    for i in range(PAIR):
                        tail_between(j, i, tail)
                        if i % 2 == 1:
                            act.wait_ge(turned, PAIR * j + i + 1)
                            nc.scalar.activation(probT[i % 4][:, :], ps_t[1][:, :], ACT.Copy).then_inc(turn_copied[1], 1)
                        if not (is_last(j) and i + AHEAD >= PAIR):
                            exp_head(j, i + AHEAD)

                for i in range(AHEAD):
                    exp_head(0, i)
                tiles(act, body, tail)
                for s in range(2):
                    act.wait_ge(x1_out[s], 16 * PAIRS)
                    act.wait_ge(tn_out[s], 16 * PAIRS)

            @block.vector
            def _(dve):
                link = Chain(dve, steps)
                wide = lambda a: a.unsqueeze(2).to_broadcast([P, TOPK, E])

                def mask_head(j, i):
                    edge = isinstance(j, int)
                    t = 2 * j + i // NH if edge else None
                    kind = 1 if t is None or 2 <= t < NT - 2 else 0 if t < 2 else 2
                    dve.wait_ge(scored, PAIR * j + i + 1)
                    wait(dve, exp_done, PAIR * j + i - 3)
                    settled(dve, passed)
                    b = i % 4
                    nc.vector.tensor_tensor_reduce(score[b][:, :], ps_s[i % NH % SB][:, :], mask[:, kind, :], 1.0, -3e38, ALU.add, ALU.max,
                                                   top[:, b:b + 1]).then_inc(masked, 1)
                    dve.wait_ge(masked, PAIR * j + i + 1)
                    nc.vector.tensor_scalar(ntop[:, b:b + 1], top[:, b:b + 1], -SCALE, None, ALU.mult).then_inc(ntop_done, 1)

                def tail(t, s, uses, step):
                    if step == 2:
                        dve.wait_ge(value_done, NH * (t + 1))
                        wait(dve, aoT_done, t)
                        link(nc.vector.reciprocal(inv[:, :], total[s][:, :]))
                        for b in range(2):
                            half = lambda a: a[:, :].rearrange("p (h b d) -> p h b d", b=2, d=HD)[:, :, b, :]
                            last = nc.vector.tensor_tensor(half(ao), half(ps_o[b]), inv[:, :].rearrange("p (h b) -> p h b", b=2)[:, :, b].unsqueeze(2)
                                                           .to_broadcast([P, NH // 2, HD]), ALU.mult)
                        last.then_inc(heads_done, 1)
                    if step == 4:
                        dve.wait_ge(projected, t + 1)
                        dve.wait_ge(xt_in[s], 16 * (uses + 1))
                        wait(dve, x1_out[s], 16 * uses)
                        nc.vector.tensor_tensor(x1[s][:, :], ps_x[:, :], xt[s][:, :], ALU.add).then_inc(x1_done, 1)
                        dve.wait_ge(x1_done, t + 1)
                        link(nc.vector.bn_stats(stats[:, :], x1[s][:, :]), passed)
                        link(nc.vector.bn_aggr(moments[:, :], stats[:, :]))
                        nc.vector.tensor_scalar(var_eps[:, :], moments[:, 1:2], EPS2, None, ALU.add).then_inc(var_done, 1)
                    if step == 5:
                        dve.wait_ge(rstd_done, t + 1)
                        wait(dve, tn_out[s], 16 * uses)
                        nc.vector.tensor_scalar(tn[s][:, :], x1[s][:, :], moments[:, 0:1], rstd[:, :], ALU.subtract, ALU.mult).then_inc(tn_done, 1)
                    if step == 7:
                        dve.wait_ge(logits_done, t + 1)
                        nc.vector.tensor_copy(logit[:, :], ps_x[:, 0:E]).then_inc(logits_read, 1)
                        dve.wait_ge(logits_read, t + 1)
                        settled(dve, passed)
                        link(nc.vector.max(big8[:, :], logit[:, :]))
                        nc.vector.tensor_scalar(nbig[:, :], big8[:, 0:1], -1.0, None, ALU.mult).then_inc(nbig_done, 1)
                    if step == 9:
                        dve.wait_ge(routed_exp, t + 1)
                        link(nc.vector.reciprocal(esum[:, :], esum[:, :]))
                        link(nc.vector.tensor_scalar(expo[:, :], expo[:, :], esum[:, :], None, ALU.mult), passed)
                        link(nc.vector.max(big8[:, :], expo[:, :]), passed)
                        link(nc.vector.max_index(index8[:, :], big8[:, :], expo[:, :]))
                        link(nc.vector.tensor_copy(index_f[:, :], index8[:, 0:TOPK]))
                    if step == 10:
                        link(nc.vector.tensor_tensor(chosen[:, :, :], k_sb[:, K_IOTA:K_IOTA + E].unsqueeze(1).to_broadcast([P, TOPK, E]),
                                                     wide(index_f[:, :]), ALU.is_equal))
                        nc.vector.tensor_reduce(taken[:, :], chosen[:, :, :].rearrange("p k e -> p e k"), AX.X, ALU.add).then_inc(taken_done, 1)
                    if step == 11:
                        link(nc.vector.tensor_reduce(gsum[:, :], big8[:, 0:TOPK], AX.X, ALU.add))
                        link(nc.vector.tensor_scalar(gsum[:, :], gsum[:, :], 1e-9, None, ALU.add))
                        link(nc.vector.reciprocal(gsum[:, :], gsum[:, :]))
                        link(nc.vector.tensor_scalar(gate6[:, :], big8[:, 0:TOPK], gsum[:, :], None, ALU.mult))
                    if step == 13:
                        dve.wait_ge(ranked, t + 1)
                        link(nc.vector.tensor_tensor(rank[:, :], ps_r[:, 0:E], counts[:, :], ALU.add))
                        link(nc.vector.tensor_tensor(counts[:, :], counts[:, :], ps_r[:, E:2 * E], ALU.add))
                        link(nc.vector.tensor_tensor(picked[:, :, :], chosen[:, :, :], rank[:, :].unsqueeze(1).to_broadcast([P, TOPK, E]), ALU.mult))
                    if step == 14:
                        link(nc.vector.tensor_reduce(slot[:, :], picked[:, :, :], AX.X, ALU.add))
                        link(nc.vector.tensor_scalar(fits[:, :], slot[:, :], float(CAP), None, ALU.is_lt))
                        link(nc.vector.scalar_tensor_tensor(row[:, :], index_f[:, :], float(CAP), slot[:, :], ALU.mult, ALU.add))
                        nc.vector.tensor_tensor(gates[:, bass.ds(t * TOPK, TOPK)], gate6[:, :], fits[:, :], ALU.mult)
                    if step == 15:
                        wait(dve, ids_out[s], 16 * TOPK * uses)
                        nc.vector.tensor_copy(experts_of[:, bass.ds(t * TOPK, TOPK)], index_f[:, :])
                        nc.vector.tensor_copy(slots_of[:, bass.ds(t * TOPK, TOPK)], slot[:, :])
                        link(nc.vector.tensor_scalar(away[:, :], fits[:, :], -FAR, FAR, ALU.mult, ALU.add))
                        link(nc.vector.tensor_tensor(row_to[s][:, :], row[:, :], away[:, :], ALU.add))
                        link(nc.vector.tensor_copy(token[s][:, :], token_f[:, :]))
                        nc.vector.tensor_scalar(token_f[:, :], token_f[:, :], float(P), None, ALU.add).then_inc(rows_done, 1)
                        dve.wait_ge(rows_done, t + 1)

                def body(j):
                    for i in range(PAIR):
                        tail_between(j, i, tail)
                        if not (is_last(j) and i + AHEAD >= PAIR):
                            mask_head(j, i + AHEAD)
                        if i % 2 == 0:
                            dve.wait_ge(turned, PAIR * j + i + 1)
                            nc.vector.tensor_copy(probT[i % 4][:, :], ps_t[0][:, :]).then_inc(turn_copied[0], 1)

                def looped_body(j):
                    if isinstance(j, int):
                        return body(j)
                    link.enter(j - 1, 2 * TAIL_STEPS)
                    body(j)
                    link.leave(j, PAIRS - 4)

                TAIL_STEPS = 23
                nc.vector.memset(ones[:, :], 1.0).then_inc(setup, 1)
                nc.vector.memset(zeros[:, :], 0).then_inc(setup, 1)
                nc.vector.memset(power[:, :], -0.5).then_inc(setup, 1)
                nc.vector.memset(counts[:, :], 0.0).then_inc(setup, 1)
                nc.vector.tensor_copy(token_f[:, :], k_sb[:, K_P:K_P + 1]).then_inc(setup, 1)
                dve.wait_ge(setup, 5)
                dve.wait_ge(w_in, 80)
                for i in range(AHEAD):
                    mask_head(0, i)
                tiles(dve, looped_body, tail)

                link(nc.vector.tensor_scalar(n_blocks[:, :], counts[:, :], 0.0, None, ALU.is_gt))
                for m in range(1, CAP // P - 1):
                    link(nc.vector.scalar_tensor_tensor(n_blocks[:, :], counts[:, :], float(m * P), n_blocks[:, :], ALU.is_gt, ALU.add))
                nc.vector.scalar_tensor_tensor(n_blocks[:, :], counts[:, :], float(CAP - P), n_blocks[:, :], ALU.is_gt, ALU.add).then_inc(blocks_done, 1)
                dve.wait_ge(map_step, 1)
                nc.vector.tensor_copy(n_blocksT[:, :], ps_x[0:E, 0:P]).then_inc(blocks_done, 1)
                dve.wait_ge(map_step, 3)
                nc.vector.tensor_scalar(starts[:, :], ps_x[:, 2 * P:2 * P + E], float(P), None, ALU.mult)
                link(nc.vector.tensor_copy(ends[:, :], ps_x[0:E, P:P + 1]))
                nc.vector.tensor_scalar(ended[:, :], k_sb[0:E, K_IOTA:K_IOTA + NB], ends[:, :], None, ALU.is_ge).then_inc(blocks_done, 1)
                dve.wait_ge(map_step, 4)
                link(nc.vector.tensor_scalar(be_f[:, :], ps_o[0][0:1, 0:NB], float(E - 1), None, ALU.min))
                link(nc.vector.tensor_copy(block_expert[:, :], be_f[:, :]))
                link(nc.vector.tensor_tensor(br_f[:, :], k_sb[0:1, K_IOTA:K_IOTA + NB], ps_t[0][0:1, 0:NB], ALU.subtract))
                link(nc.vector.tensor_scalar(br_f[:, :], br_f[:, :], float(P), None, ALU.mult))
                nc.vector.scalar_tensor_tensor(block_row[:, :], ps_o[0][0:1, 0:NB], float(CAP), br_f[:, :], ALU.mult, ALU.add).then_inc(map_done, 1)

            @block.gpsimd
            def _(pool):
                def power_half(t):
                    pool.wait_ge(var_done, t + 1)
                    nc.gpsimd.tensor_tensor(rstd[:, :], var_eps[:, :], power[:, :], ALU.pow).then_inc(rstd_done, 1)

                def send_ids(t, s):
                    pool.wait_ge(rows_done, t + 1)
                    settled(pool, passed_pool)
                    for c in range(TOPK):
                        nc.gpsimd.indirect_dma_start(out=ids_d, out_offset=bass.IndirectOffsetOnAxis(row_to[s][:, c:c + 1], 0),
                                                     in_=token[s][:, :], in_offset=None, bounds_check=E * CAP - 1,
                                                     oob_is_err=False).then_inc(ids_out[s], 16)

                pool.wait_ge(setup, 5)
                pool.wait_ge(zeroed, 16)
                power_half(0)

                def turn(j):
                    for s in range(2):
                        power_half(2 * j + s + 1)
                        send_ids(2 * j + s, s)

                turns(pool, PAIRS - 1, turn)
                power_half(NT - 1)
                for s in range(2):
                    send_ids(NT - 2 + s, s)
                for s in range(2):
                    pool.wait_ge(ids_out[s], 16 * TOPK * PAIRS)


def pipeline(eng, width, count, first, step, last, link=None, links=0):
    first()
    for s in range(1, width):
        step(0, s)
    with eng.Fori(1, count - 1) as j:
        if link is not None:
            link.enter(j, links)
        for s in range(width):
            step(j, s)
        if link is not None:
            link.leave(j, count - 2)
    for s in range(width - 1):
        step(count - 1, s)
    last()


def expert_blocks(nc, experts, tn_d, ids_d, rows_d, k_sb, block_expert, block_row):
    UP, DOWN = CC * 2 * F, FC * C
    with ExitStack() as ctx:
        sb = lambda n, s, d=fp32: ctx.enter_context(nc.sbuf_tensor(n, s, d))
        sem = lambda n: ctx.enter_context(nc.semaphore("d_" + n))
        ps = lambda n: ctx.enter_context(nc.psum_tensor(n, [P, CH], fp32))
        w = [sb(f"w{s}", [P, UP + DOWN]) for s in range(4)]
        ids = [sb(f"ids{s}", [P, 1], i32) for s in range(4)]
        xg = [sb(f"xg{s}", [P, C]) for s in range(4)]
        xT = [sb(f"xT{s}", [P, C]) for s in range(2)]
        sg = [sb(f"sg{s}", [P, F]) for s in range(2)]
        h = [sb(f"h{s}", [P, F]) for s in range(2)]
        hT = [sb(f"hT{s}", [P, F]) for s in range(2)]
        y = [sb(f"y{s}", [P, C]) for s in range(4)]
        ps_x, ps_u, ps_h, ps_y = [[ps(f"{n}{s}") for s in range(2)] for n in ("ps_x", "ps_u", "ps_h", "ps_y")]
        w_in, ids_in, x_in, y_out = [[sem(f"{n}{s}") for s in range(4)] for n in ("w_in", "ids_in", "x_in", "y_out")]
        x_turned, x_copied, up_done, silu_done, h_done, h_turned, h_copied, down_done, y_copied = [
            sem(n) for n in ("x_turned", "x_copied", "up_done", "silu_done", "h_done", "h_turned", "h_copied", "down_done", "y_copied")]
        passed, passed_pool = sem("passed"), sem("passed_pool")
        R = 4
        TURNS = NB // R

        with nc.Block() as block:
            @block.sync
            def _(sp):
                def load(j):
                    for s in range(R):
                        b = R * j + s
                        expert = sp.value_load(block_expert[0:1, bass.ds(b, 1)], min_val=0, max_val=E - 1)
                        row = sp.value_load(block_row[0:1, bass.ds(b, 1)], min_val=0, max_val=SLOTS - P)
                        wait(sp, x_in[s], 16 * j)
                        settled(sp, passed)
                        sp.dma_start(ids[s][:, :], ids_d[bass.ds(row, P), :]).then_inc(ids_in[s], 16)
                        wait(sp, down_done, b - R + 1)
                        settled(sp, passed)
                        sp.dma_start(w[s][:, :], experts[bass.ds(expert, 1), :, :].rearrange("a p n -> (a p) n")).then_inc(w_in[s], 16)

                turns(sp, TURNS, load)

            @block.gpsimd
            def _(pool):
                def fetch(j):
                    for s in range(R):
                        pool.wait_ge(ids_in[s], 16 * j + 16)
                        wait(pool, x_turned, R * j + s - R + 1)
                        settled(pool, passed_pool)
                        nc.gpsimd.indirect_dma_start(out=xg[s][:, :], out_offset=None, in_=tn_d,
                                                     in_offset=bass.IndirectOffsetOnAxis(ids[s][:, :], 0)).then_inc(x_in[s], 16)

                turns(pool, TURNS, fetch)

            @block.tensor
            def _(pe):
                ident = k_sb[:, K_ID:K_ID + P]

                def turn_x(j, i):
                    s = i % R
                    b = R * j + i
                    pe.wait_ge(x_in[s], 16 * (j + i // R + 1))
                    wait(pe, x_copied, b - 1)
                    for c in range(CC):
                        at = slice(c * P, (c + 1) * P)
                        last = nc.tensor.transpose(ps_x[i % 2][:, at], xg[s][:, at], ident)
                    last.then_inc(x_turned, 1)

                def up(j, s):
                    b = R * j + s
                    pe.wait_ge(x_copied, b + 1)
                    pe.wait_ge(w_in[s], 16 * (j + 1))
                    wait(pe, h_done, b - 1)
                    for c in range(CC):
                        last = nc.tensor.matmul(ps_u[s % 2][:, :], xT[s % 2][:, c * P:(c + 1) * P], w[s][:, c * 2 * F:(c + 1) * 2 * F],
                                                start=c == 0, stop=c == CC - 1)
                    last.then_inc(up_done, 1)

                def turn_h(j, i):
                    b = R * j + i
                    pe.wait_ge(h_done, b + 1)
                    wait(pe, h_copied, b - 1)
                    for c in range(FC):
                        at = slice(c * P, (c + 1) * P)
                        last = nc.tensor.transpose(ps_h[i % 2][:, at], h[i % 2][:, at], ident)
                    last.then_inc(h_turned, 1)

                def down(j, i):
                    b = R * j + i
                    pe.wait_ge(h_copied, b + 1)
                    wait(pe, y_copied, b - 1)
                    for c in range(FC):
                        last = nc.tensor.matmul(ps_y[i % 2][:, :], hT[i % 2][:, c * P:(c + 1) * P], w[i % R][:, UP + c * C:UP + (c + 1) * C],
                                                start=c == 0, stop=c == FC - 1)
                    last.then_inc(down_done, 1)

                def first():
                    turn_x(0, 0)
                    up(0, 0)
                    turn_x(0, 1)

                def step(j, s):
                    turn_h(j, s - 1)
                    up(j, s)
                    turn_x(j, s + 1)
                    down(j, s - 1)

                def last():
                    turn_h(TURNS - 1, R - 2)
                    up(TURNS - 1, R - 1)
                    down(TURNS - 1, R - 2)
                    turn_h(TURNS - 1, R - 1)
                    down(TURNS - 1, R - 1)

                pipeline(pe, R, TURNS, first, step, last)

            @block.scalar
            def _(act):
                def copy_h(j, i):
                    act.wait_ge(h_turned, R * j + i + 1)
                    nc.scalar.activation(hT[i % 2][:, :], ps_h[i % 2][:, 0:F], ACT.Copy).then_inc(h_copied, 1)

                def silu(j, s):
                    act.wait_ge(up_done, R * j + s + 1)
                    wait(act, h_done, R * j + s - 1)
                    nc.scalar.activation(sg[s % 2][:, :], ps_u[s % 2][:, 0:F], ACT.Silu).then_inc(silu_done, 1)

                def copy_y(j, i):
                    b = R * j + i
                    act.wait_ge(down_done, b + 1)
                    uses = j + i // R
                    wait(act, y_out[i % R], 16 * uses)
                    nc.scalar.activation(y[i % R][:, :], ps_y[i % 2][:, :], ACT.Copy).then_inc(y_copied, 1)
                    act.wait_ge(y_copied, b + 1)
                    act.dma_start(rows_d[bass.ds(b * P, P), :], y[i % R][:, :]).then_inc(y_out[i % R], 16)

                def first():
                    silu(0, 0)

                def step(j, s):
                    copy_h(j, s - 1)
                    silu(j, s)
                    copy_y(j, s - 1)

                def last():
                    step(TURNS - 1, R - 1)
                    copy_h(TURNS - 1, R - 1)
                    copy_y(TURNS - 1, R - 1)

                pipeline(act, R, TURNS, first, step, last)
                for s in range(R):
                    act.wait_ge(y_out[s], 16 * TURNS)

            @block.vector
            def _(dve):
                def copy_x(j, i):
                    dve.wait_ge(x_turned, R * j + i + 1)
                    nc.vector.tensor_copy(xT[i % 2][:, :], ps_x[i % 2][:, :]).then_inc(x_copied, 1)

                def gated(j, s):
                    dve.wait_ge(silu_done, R * j + s + 1)
                    nc.vector.tensor_tensor(h[s % 2][:, :], sg[s % 2][:, :], ps_u[s % 2][:, F:2 * F], ALU.mult).then_inc(h_done, 1)

                def first():
                    copy_x(0, 0)
                    gated(0, 0)
                    copy_x(0, 1)

                def step(j, s):
                    gated(j, s)
                    copy_x(j, s + 1)

                def last():
                    gated(TURNS - 1, R - 1)

                pipeline(dve, R, TURNS, first, step, last)


def shared_and_combine(nc, sh_up, sh_down, tn_d, x1_d, rows_d, out, k_sb, gates, experts_of, slots_of, starts):
    tn_v, x1_v, out_v = (a.rearrange("(t p) c -> t p c", p=P) for a in (tn_d, x1_d, out))
    one_tile = lambda a, t: a[bass.ds(t, 1), :, :].rearrange("a p n -> (a p) n")
    SH = 2 * F
    SC = SH // P
    PAIRS = NT // 2
    with ExitStack() as ctx:
        sb = lambda n, s, d=fp32: ctx.enter_context(nc.sbuf_tensor(n, s, d))
        sem = lambda n: ctx.enter_context(nc.semaphore("e_" + n))
        ps = lambda n: ctx.enter_context(nc.psum_tensor(n, [P, CH], fp32))
        up, down = sb("up", [P, CC, 2 * SH]), sb("down", [P, SC, C])
        tn = [sb(f"tn_{s}", [P, C]) for s in range(2)]
        x1 = [sb(f"x1_{s}", [P, C]) for s in range(2)]
        got = [[sb(f"got{s}{c}", [P, C]) for c in range(TOPK)] for s in range(2)]
        place = [sb(f"place{s}", [P, TOPK], i32) for s in range(2)]
        gate = [sb(f"gate{s}", [P, TOPK]) for s in range(2)]
        chosen, slot, row, spare_row = sb("chosen_", [P, TOPK, E]), sb("slot_", [P, TOPK]), sb("row_", [P, TOPK]), sb("spare_row", [P, 1])
        tnT, sg, h, hT, o = [[sb(f"{n}{s}", [P, C]) for s in range(2)] for n in ("tnT_", "sg_", "h_", "hT_", "o")]
        ps_x, ps_h = ps("ps_x_"), ps("ps_h_")
        ps_g, ps_u, ps_y = [[ps(f"{n}{s}") for s in range(2)] for n in ("ps_g_", "ps_u_", "ps_y_")]
        tn_in, x1_in, rows_in, stored = [[sem(f"{n}{s}") for s in range(2)] for n in ("tn_in", "x1_in", "rows_in", "stored")]
        w_in, setup, placed, tn_turned, tn_copied, up_done, silu_done, h_done, h_turned, h_copied, down_done, shared_in, dve_steps, done = [
            sem(n) for n in ("w_in", "setup", "placed", "tn_turned", "tn_copied", "up_done", "silu_done", "h_done", "h_turned", "h_copied",
                             "down_done", "shared_in", "dve_steps", "done")]
        passed = sem("passed")

        with nc.Block() as block:
            @block.sync
            def _(sp):
                sp.dma_start(up[:, :, :], sh_up).then_inc(w_in, 16)
                sp.dma_start(down[:, :, :], sh_down).then_inc(w_in, 16)

                def turn(j):
                    for s in range(2):
                        wait(sp, tn_turned, 2 * j + s - 1)
                        sp.dma_start(tn[s][:, :], one_tile(tn_v, 2 * j + s)).then_inc(tn_in[s], 16)
                        wait(sp, shared_in, 2 * j + s - 1)
                        sp.dma_start(x1[s][:, :], one_tile(x1_v, 2 * j + s)).then_inc(x1_in[s], 16)

                turns(sp, PAIRS, turn)

            @block.gpsimd
            def _(pool):
                def turn(j):
                    for s in range(2):
                        pool.wait_ge(placed, 2 * j + s + 1)
                        settled(pool, passed)
                        for c in range(TOPK):
                            nc.gpsimd.indirect_dma_start(out=got[s][c][:, :], out_offset=None, in_=rows_d,
                                                         in_offset=bass.IndirectOffsetOnAxis(place[s][:, c:c + 1], 0)).then_inc(rows_in[s], 16)

                turns(pool, PAIRS, turn)

            @block.tensor
            def _(pe):
                ident = k_sb[:, K_ID:K_ID + P]

                def turn_tokens(j, i):
                    t = 2 * j + i
                    pe.wait_ge(tn_in[i % 2], 16 * (j + i // 2 + 1))
                    wait(pe, tn_copied, t)
                    for c in range(CC):
                        at = slice(c * P, (c + 1) * P)
                        last = nc.tensor.transpose(ps_x[:, at], tn[i % 2][:, at], ident)
                    last.then_inc(tn_turned, 1)

                def go_up(j, s):
                    t = 2 * j + s
                    pe.wait_ge(tn_copied, t + 1)
                    wait(pe, h_done, t - 1)
                    for bank, at in ((ps_g[s], 0), (ps_u[s], SH)):
                        for c in range(CC):
                            last = nc.tensor.matmul(bank[:, :], tnT[s][:, c * P:(c + 1) * P], up[:, c, at:at + SH], start=c == 0, stop=c == CC - 1)
                        last.then_inc(up_done, 1)

                def turn_hidden(j, i):
                    t = 2 * j + i
                    pe.wait_ge(h_done, t + 1)
                    wait(pe, h_copied, t)
                    for c in range(SC):
                        at = slice(c * P, (c + 1) * P)
                        last = nc.tensor.transpose(ps_h[:, at], h[i % 2][:, at], ident)
                    last.then_inc(h_turned, 1)

                def go_down(j, i):
                    t = 2 * j + i
                    pe.wait_ge(h_copied, t + 1)
                    wait(pe, shared_in, t - 1)
                    for c in range(SC):
                        last = nc.tensor.matmul(ps_y[i % 2][:, :], hT[i % 2][:, c * P:(c + 1) * P], down[:, c, :], start=c == 0, stop=c == SC - 1)
                    last.then_inc(down_done, 1)

                def first():
                    turn_tokens(0, 0)
                    pe.wait_ge(w_in, 32)
                    go_up(0, 0)
                    turn_tokens(0, 1)

                def step(j, s):
                    turn_hidden(j, s - 1)
                    go_up(j, s)
                    turn_tokens(j, s + 1)
                    go_down(j, s - 1)

                def last():
                    turn_hidden(PAIRS - 1, 0)
                    go_up(PAIRS - 1, 1)
                    go_down(PAIRS - 1, 0)
                    turn_hidden(PAIRS - 1, 1)
                    go_down(PAIRS - 1, 1)

                pipeline(pe, 2, PAIRS, first, step, last)

            @block.scalar
            def _(act):
                def copy_tokens(j, i):
                    t = 2 * j + i
                    act.wait_ge(tn_turned, t + 1)
                    wait(act, up_done, 2 * t - 2)
                    nc.scalar.activation(tnT[i % 2][:, :], ps_x[:, :], ACT.Copy).then_inc(tn_copied, 1)

                def silu(j, s):
                    t = 2 * j + s
                    act.wait_ge(up_done, 2 * t + 1)
                    wait(act, h_done, t - 1)
                    nc.scalar.activation(sg[s][:, :], ps_g[s][:, :], ACT.Silu).then_inc(silu_done, 1)

                def copy_hidden(j, i):
                    t = 2 * j + i
                    act.wait_ge(h_turned, t + 1)
                    wait(act, down_done, t - 1)
                    nc.scalar.activation(hT[i % 2][:, :], ps_h[:, :], ACT.Copy).then_inc(h_copied, 1)

                def store(j, i):
                    act.wait_ge(done, 2 * j + i + 1)
                    act.dma_start(one_tile(out_v, 2 * j + i), o[i % 2][:, :]).then_inc(stored[i % 2], 16)

                def first():
                    copy_tokens(0, 0)
                    silu(0, 0)
                    copy_tokens(0, 1)

                def step(j, s):
                    copy_hidden(j, s - 1)
                    silu(j, s)
                    copy_tokens(j, s + 1)
                    if not (isinstance(j, int) and j == 0):
                        store(j, s - 2)

                def last():
                    copy_hidden(PAIRS - 1, 0)
                    silu(PAIRS - 1, 1)
                    store(PAIRS - 1, -1)
                    copy_hidden(PAIRS - 1, 1)
                    store(PAIRS - 1, 0)
                    store(PAIRS - 1, 1)

                pipeline(act, 2, PAIRS, first, step, last)
                for s in range(2):
                    act.wait_ge(stored[s], 16 * PAIRS)

            @block.vector
            def _(dve):
                link = Chain(dve, dve_steps)
                nc.vector.tensor_scalar(spare_row[:, :], k_sb[:, K_P:K_P + 1], float((NB - 1) * P), None, ALU.add).then_inc(setup, 1)
                dve.wait_ge(setup, 1)

                def place_rows(j, i):
                    t, s = 2 * j + i, i % 2
                    at = bass.ds(t * TOPK, TOPK)
                    nc.vector.tensor_copy(gate[s][:, :], gates[:, at])
                    link(nc.vector.tensor_copy(slot[:, :], slots_of[:, at]))
                    link(nc.vector.tensor_tensor(chosen[:, :, :], k_sb[:, K_IOTA:K_IOTA + E].unsqueeze(1).to_broadcast([P, TOPK, E]),
                                                 experts_of[:, at].unsqueeze(2).to_broadcast([P, TOPK, E]), ALU.is_equal))
                    link(nc.vector.tensor_tensor(chosen[:, :, :], chosen[:, :, :], starts[:, :].unsqueeze(1).to_broadcast([P, TOPK, E]), ALU.mult))
                    link(nc.vector.tensor_reduce(row[:, :], chosen[:, :, :], AX.X, ALU.add))
                    link(nc.vector.tensor_tensor(row[:, :], row[:, :], slot[:, :], ALU.add))
                    link(nc.vector.tensor_scalar(slot[:, :], slot[:, :], float(CAP), None, ALU.is_lt))
                    link(nc.vector.scalar_tensor_tensor(row[:, :], row[:, :], spare_row[:, :], slot[:, :], ALU.subtract, ALU.mult))
                    nc.vector.tensor_scalar(place[s][:, :], row[:, :], spare_row[:, :], None, ALU.add).then_inc(placed, 1)
                    dve.wait_ge(placed, t + 1)

                def gated(j, s):
                    t = 2 * j + s
                    dve.wait_ge(silu_done, t + 1)
                    dve.wait_ge(up_done, 2 * t + 2)
                    wait(dve, h_turned, t - 1)
                    nc.vector.tensor_tensor(h[s][:, :], sg[s][:, :], ps_u[s][:, :], ALU.mult).then_inc(h_done, 1)

                def combine(j, i):
                    t, s, turn = 2 * j + i, i % 2, j + i // 2
                    dve.wait_ge(down_done, t + 1)
                    dve.wait_ge(x1_in[s], 16 * turn + 16)
                    wait(dve, stored[s], 16 * turn)
                    nc.vector.scalar_tensor_tensor(o[s][:, :], ps_y[s][:, :], 0.5, x1[s][:, :], ALU.mult, ALU.add).then_inc(shared_in, 1)
                    dve.wait_ge(shared_in, t + 1)
                    dve.wait_ge(rows_in[s], 16 * TOPK * (turn + 1))
                    for c in range(TOPK):
                        add = nc.vector.scalar_tensor_tensor(o[s][:, :], got[s][c][:, :], gate[s][:, c:c + 1], o[s][:, :], ALU.mult, ALU.add)
                        if c < TOPK - 1:
                            link(add)
                    add.then_inc(done, 1)
                    dve.wait_ge(done, t + 1)

                def first():
                    place_rows(0, 0)
                    gated(0, 0)
                    place_rows(0, 1)

                def step(j, s):
                    gated(j, s)
                    combine(j, s - 1)
                    place_rows(j, s + 1)

                def last():
                    gated(PAIRS - 1, 1)
                    combine(PAIRS - 1, 0)
                    combine(PAIRS - 1, 1)

                pipeline(dve, 2, PAIRS, first, step, last, link, 2 * (TOPK - 1 + 7))


def program(nc, x, x_tok, pos, freq, w_qkv, taps, w_out, b_out, router_w, router_b, sh_up, sh_down, experts, masks, consts, out):
    dram = lambda n, s, d=fp32: nc.dram_tensor(n, s, d, kind="Internal").ap()
    cos_d, sin_d = dram("cos_d", [P, N]), dram("sin_d", [P, N])
    qk_d = dram("qk_d", [2 * CC, P, N])
    v_d = dram("v_d", [N, C])
    x1_d, tn_d = dram("x1_d", [N, C]), dram("tn_d", [N, C])
    ids_d = dram("ids_d", [SLOTS, 1], i32)
    rows_d = dram("rows_d", [NB * P, C])
    with ExitStack() as ctx:
        sb = lambda n, s, d=fp32: ctx.enter_context(nc.sbuf_tensor(n, s, d))
        k_sb = sb("k_sb", [P, K_END])
        gates, experts_of, slots_of = [sb(n, [P, NT * TOPK]) for n in ("gates", "experts_of", "slots_of")]
        starts = sb("starts", [P, E])
        block_expert = sb("block_expert", [1, NB], i32)
        block_row = sb("block_row", [1, NB], i32)
        k_in = ctx.enter_context(nc.semaphore("k_in"))
        with nc.Block() as block:
            @block.sync
            def _(sp):
                sp.dma_start(k_sb[:, :], consts).then_inc(k_in, 16)
                sp.wait_ge(k_in, 16)
        with nc.sbuf_tensor("xn", [P, CC, N], fp32) as xn:
            layernorm_and_tables(nc, x, pos, freq, cos_d, sin_d, xn)
            qkv_conv_rotary(nc, w_qkv, taps, cos_d, sin_d, qk_d, v_d, xn, k_sb)
        if True:
            attention_and_routing(nc, x_tok, masks, w_out, b_out, router_w, router_b, qk_d, v_d, x1_d, tn_d, ids_d,
                                  k_sb, gates, experts_of, slots_of, starts, block_expert, block_row)
        if True:
            expert_blocks(nc, experts, tn_d, ids_d, rows_d, k_sb, block_expert, block_row)
        if True:
            shared_and_combine(nc, sh_up, sh_down, tn_d, x1_d, rows_d, out, k_sb, gates, experts_of, slots_of, starts)


def shape_constants():
    import numpy as np
    k = np.zeros((P, K_END), np.float32)
    i = np.arange(P)
    k[:, K_ID:K_ID + P] = i[:, None] == i[None, :]
    k[:, K_BEFORE:K_BEFORE + P] = i[:, None] < i[None, :]
    k[:E, K_UPTO:K_UPTO + E] = i[:E, None] <= i[None, :E]
    k[:, K_IOTA:K_IOTA + NB] = np.arange(NB)
    k[:, K_P] = i
    for h in range(P // HD):
        for r in range(RH):
            a = h * HD + r
            k[a + RH, K_ROT + a] = -1.0
            k[a, K_ROT + a + RH] = 1.0
    row, col = i // IMG, i % IMG
    first_col = np.clip(col - KW // 2, 0, IMG - KW)
    key_row, key_col = np.arange(WIN) // IMG, np.arange(WIN) % IMG
    in_cols = (key_col[None] >= first_col[:, None]) & (key_col[None] < first_col[:, None] + KW)
    masks = []
    for first_row in (0 * row, row, 0 * row + 1):
        in_rows = (key_row[None] >= first_row[:, None]) & (key_row[None] < first_row[:, None] + KW)
        masks.append(np.where(in_rows & in_cols, 0.0, -1e30))
    return k, np.stack(masks).astype(np.float32)


def layout(x, L0_conv_pos, L0_conv_w_qkv, L0_conv_w_dw, L0_conv_b_dw, L0_conv_freqs, L0_conv_w_out, L0_conv_b_out,
           L0_ffn_router_w, L0_ffn_bias, L0_ffn_shared_w_gate, L0_ffn_shared_w_up, L0_ffn_shared_w_down,
           L0_ffn_w_gate, L0_ffn_w_up, L0_ffn_w_down):
    import numpy as np
    k, masks = shape_constants()
    img = np.asarray(x).reshape(C, N)
    pos = np.asarray(L0_conv_pos).reshape(N, 2).T
    pos = np.broadcast_to(pos[None, :, None, :], (NH, 2, RH // 2, N)).reshape(P, N)
    freq = np.broadcast_to(np.asarray(L0_conv_freqs)[:, None, :], (NH, 2, RH // 2)).reshape(P, 1)
    order = [o for h in range(CC) for o in (h, CC + h)] + [2 * CC + h for h in range(CC)]
    w_qkv = np.asarray(L0_conv_w_qkv).reshape(3 * CC, P, CC, P)[order].transpose(0, 3, 2, 1)
    taps = np.concatenate([np.asarray(L0_conv_w_dw).reshape(3 * CC, P, TAPS), np.asarray(L0_conv_b_dw).reshape(3 * CC, P, 1)], 2)[order]
    chunks = lambda w: w.reshape(-1, P, w.shape[-1]).transpose(1, 0, 2)
    w_out = chunks(np.asarray(L0_conv_w_out).T)
    router = chunks(np.asarray(L0_ffn_router_w).T)
    gate, up = (np.asarray(w).reshape(2 * F, C).T for w in (L0_ffn_shared_w_gate, L0_ffn_shared_w_up))
    sh_up = np.concatenate([chunks(gate), chunks(up)], 2)
    sh_down = chunks(np.asarray(L0_ffn_shared_w_down).transpose(0, 2, 1).reshape(2 * F, C))
    wg, wu = (np.asarray(w).transpose(0, 2, 1).reshape(E, CC, P, F) for w in (L0_ffn_w_gate, L0_ffn_w_up))
    up_both = np.concatenate([wg, wu], 3).transpose(0, 2, 1, 3).reshape(E, P, CC * 2 * F)
    down = np.asarray(L0_ffn_w_down).transpose(0, 2, 1).reshape(E, FC, P, C).transpose(0, 2, 1, 3).reshape(E, P, FC * C)
    return {
        "x": img, "x_tok": img.T, "pos": pos, "freq": freq, "w_qkv": w_qkv, "taps": taps, "w_out": w_out,
        "b_out": np.asarray(L0_conv_b_out).reshape(1, C), "router_w": router,
        "router_b": np.asarray(L0_ffn_bias).reshape(1, E), "sh_up": sh_up, "sh_down": sh_down,
        "experts": np.concatenate([up_both, down], 2), "masks": masks, "consts": k,
    }


def kernel(**inputs):
    import numpy as np
    import concourse.bacc as bacc
    from concourse.bass_utils import run_bass_kernel_spmd

    arrays = {n: np.ascontiguousarray(a) for n, a in layout(**inputs).items()}
    nc = bacc.Bacc("TRN2", target_bir_lowering=False, num_devices=1)
    args = {n: nc.dram_tensor("in_" + n, a.shape, mybir.dt.from_np(a.dtype), kind="ExternalInput").ap() for n, a in arrays.items()}
    out = nc.dram_tensor("out_tok", [N, C], fp32, kind="ExternalOutput").ap()
    program(nc, out=out, **args)
    r = run_bass_kernel_spmd(nc, [{"in_" + n: a for n, a in arrays.items()}], core_ids=[0])
    return np.ascontiguousarray(r.results[0]["out_tok"].T).reshape(1, C, IMG, IMG)
```

```python
import concourse.bass as bass
from concourse import mybir
from contextlib import ExitStack

fp32 = mybir.dt.float32
i32 = mybir.dt.int32
u32 = mybir.dt.uint32
ALU = mybir.AluOpType
ACT = mybir.ActivationFunctionType
AX = mybir.AxisListType

C = 512
IMG = 64
N = IMG * IMG
P = 128
CC = C // P
CH = 512
NCH = N // CH
NH = 8
HD = C // NH
RH = 16
KW = 7
WROWS = 8
WIN = WROWS * IMG
NT = N // P
TAPS = 9
E = 64
F = 256
FC = F // P
SH = 2 * F
SC = SH // P
TOPK = 6
CAP = int(N * TOPK * 2.0 / E)
NB = 256
SLOTS = E * CAP + NB * P
FAR = 4.0 * SLOTS
PAD = IMG + 2
SCALE = HD ** -0.5
EPS1, EPS2 = 1e-6, 1e-5
PI = 3.1415925
TWO_PI = 6.283185307179586
PI_A = 6.28125
PI_B = 0.0019350051879882812
PI_C = TWO_PI - PI_A - PI_B
ROUND = 12582912.0
TURN, W_SLOTS = 4, 4
ROUND_DOWN = 3 / 8

K_ID, K_BEFORE, K_UPTO, K_IOTA, K_P, K_ROT, K_END = 0, 128, 256, 320, 576, 577, 705


def wait(eng, sem, value):
    if isinstance(value, int) and value <= 0:
        return
    eng.wait_ge(sem, value)


def settled(eng, passed):
    eng.sem_inc(passed, 1)


def turns(eng, count, turn):
    turn(0)
    with eng.Fori(1, count) as j:
        turn(j)


class Chain:

    def __init__(self, eng, sem):
        self.eng, self.sem, self.before, self.base, self.n = eng, sem, 0, 0, 0

    def __call__(self, ins, passed=None):
        ins.then_inc(self.sem, 1)
        self.n += 1
        self.eng.wait_ge(self.sem, self.base + self.n)
        if passed is not None:
            settled(self.eng, passed)

    def enter(self, j, steps):
        self.before, self.steps = self.base + self.n, steps
        if not isinstance(j, int):
            self.base, self.n = (j - 1) * steps + self.before, 0

    def leave(self, j, looped):
        assert self.base + self.n == self.before + self.steps if isinstance(j, int) else self.n == self.steps
        if not isinstance(j, int):
            self.base, self.n = self.before + looped * self.steps, 0


def layernorm_and_tables(nc, x, pos, freq, cos_d, sin_d, xn):
    SLOTS_X = 4
    xv = x.rearrange("(c p) n -> p c n", p=P)
    with ExitStack() as ctx:
        sb = lambda n, s, d=fp32: ctx.enter_context(nc.sbuf_tensor(n, s, d))
        sem = lambda n: ctx.enter_context(nc.semaphore("a_" + n))
        ps = lambda n: ctx.enter_context(nc.psum_tensor(n, [P, CH], fp32))
        xc = [sb(f"xc{s}", [P, CC, CH]) for s in range(SLOTS_X)]
        sq = [sb(f"sq{s}", [P, CC, CH]) for s in range(2)]
        var = [sb(f"var{s}", [P, CH]) for s in range(2)]
        dev, newton = [[sb(f"{n}{s}", [P, CH]) for s in range(2)] for n in ("dev", "newton")]
        mean_w = sb("mean_w", [P, P])
        eps = sb("eps1", [P, 1])
        fr = sb("fr", [P, 1])
        th = sb("th", [P, N])
        half = sb("half", [P, N])
        whole = sb("whole", [P, N])
        ps_m, ps_v = [[ps(f"{n}{s}") for s in range(2)] for n in ("ps_m", "ps_v")]
        x_in = [sem(f"x_in{s}") for s in range(SLOTS_X)]
        pos_in, setup, mean_done, centred, squared = [
            sem(n) for n in ("pos_in", "setup", "mean_done", "centred", "squared")]
        var_done, var_copied, dev_done, inverted, newton_step, rstd_done, normed, steps, angles, sines = [
            sem(n) for n in ("var_done", "var_copied", "dev_done", "inverted", "newton_step", "rstd_done", "normed", "dve_steps", "angles", "sines")]
        sin_out, cos_out = sem("sin_out"), sem("cos_out")

        with nc.Block() as block:
            @block.sync
            def _(sp):
                for t in range(NCH):
                    wait(sp, normed, t - SLOTS_X + 1)
                    sp.dma_start(xc[t % SLOTS_X][:, :, :], xv[:, :, t * CH:(t + 1) * CH]).then_inc(x_in[t % SLOTS_X], 16)
                    if t == 1:
                        sp.dma_start(th[:, :], pos).then_inc(pos_in, 16)
                        sp.dma_start(fr[:, :], freq).then_inc(pos_in, 16)
                sp.wait_ge(sines, 1)
                sp.dma_start(sin_d, half[:, :]).then_inc(sin_out, 16)
                sp.wait_ge(sines, 2)
                sp.dma_start(cos_d, th[:, :]).then_inc(cos_out, 16)
                sp.wait_ge(sin_out, 16)
                sp.wait_ge(cos_out, 16)

            @block.tensor
            def _(pe):
                def mean(t):
                    pe.wait_ge(x_in[t % SLOTS_X], 16 * (t // SLOTS_X + 1))
                    wait(pe, centred, t - 1)
                    for c in range(CC):
                        last = nc.tensor.matmul(ps_m[t % 2][:, :], mean_w[:, :], xc[t % SLOTS_X][:, c, :], start=c == 0, stop=c == CC - 1)
                    last.then_inc(mean_done, 1)

                def variance(t):
                    pe.wait_ge(squared, t + 1)
                    wait(pe, dev_done, t - 1)
                    for c in range(CC):
                        last = nc.tensor.matmul(ps_v[t % 2][:, :], mean_w[:, :], sq[t % 2][:, c, :], start=c == 0, stop=c == CC - 1)
                    last.then_inc(var_done, 1)

                pe.wait_ge(setup, 2)
                mean(0)
                for t in range(1, NCH):
                    mean(t)
                    variance(t - 1)
                variance(NCH - 1)

            @block.scalar
            def _(act):
                def square(t):
                    act.wait_ge(centred, t + 1)
                    wait(act, var_done, t - 1)
                    nc.scalar.activation(sq[t % 2][:, :, :], xc[t % SLOTS_X][:, :, :], ACT.Square).then_inc(squared, 1)

                def deviation(t):
                    act.wait_ge(var_done, t + 1)
                    wait(act, rstd_done, t - 1)
                    wait(act, normed, t - 1)
                    nc.scalar.activation(var[t % 2][:, :], ps_v[t % 2][:, :], ACT.Identity, bias=eps[:, :]).then_inc(var_copied, 1)
                    nc.scalar.activation(dev[t % 2][:, :], ps_v[t % 2][:, :], ACT.Sqrt, bias=eps[:, :]).then_inc(dev_done, 1)

                act.wait_ge(setup, 2)
                square(0)
                for t in range(1, NCH):
                    square(t)
                    deviation(t - 1)
                deviation(NCH - 1)
                act.wait_ge(angles, 1)
                nc.scalar.activation(half[:, :], half[:, :], ACT.Sin).then_inc(sines, 1)
                act.wait_ge(angles, 2)
                nc.scalar.activation(th[:, :], th[:, :], ACT.Sin).then_inc(sines, 1)

            @block.gpsimd
            def _(pool):
                for t in range(NCH):
                    d, n, v = dev[t % 2][:, :], newton[t % 2][:, :], var[t % 2][:, :]
                    pool.wait_ge(inverted, t + 1)
                    nc.gpsimd.tensor_tensor(n, d, d, ALU.mult).then_inc(newton_step, 1)
                    pool.wait_ge(newton_step, 3 * t + 1)
                    pool.wait_ge(var_copied, t + 1)
                    nc.gpsimd.tensor_tensor(n, n, v, ALU.mult).then_inc(newton_step, 1)
                    pool.wait_ge(newton_step, 3 * t + 2)
                    nc.gpsimd.tensor_scalar(n, n, -0.5, 1.5, ALU.mult, ALU.add).then_inc(newton_step, 1)
                    pool.wait_ge(newton_step, 3 * t + 3)
                    nc.gpsimd.tensor_tensor(d, d, n, ALU.mult).then_inc(rstd_done, 1)
                    pool.wait_ge(rstd_done, t + 1)

            @block.vector
            def _(dve):
                link = Chain(dve, steps)
                over_channels = lambda a: a.unsqueeze(1).to_broadcast([P, CC, CH])
                nc.vector.memset(mean_w[:, :], 1.0 / C).then_inc(setup, 1)
                nc.vector.memset(eps[:, :], EPS1).then_inc(setup, 1)

                def centre(t):
                    dve.wait_ge(mean_done, t + 1)
                    x_t = xc[t % SLOTS_X][:, :, :]
                    nc.vector.tensor_tensor(x_t, x_t, over_channels(ps_m[t % 2][:, :]), ALU.subtract).then_inc(centred, 1)

                def invert(t):
                    dve.wait_ge(dev_done, t + 1)
                    nc.vector.reciprocal(dev[t % 2][:, :], dev[t % 2][:, :]).then_inc(inverted, 1)

                def scale(t):
                    dve.wait_ge(rstd_done, t + 1)
                    nc.vector.tensor_tensor(xn[:, :, t * CH:(t + 1) * CH], xc[t % SLOTS_X][:, :, :], over_channels(dev[t % 2][:, :]), ALU.mult).then_inc(normed, 1)

                def turn_angles(step):
                    if step == 0:
                        dve.wait_ge(pos_in, 32)
                        link(nc.vector.tensor_scalar(th[:, :], th[:, :], fr[:, :], None, ALU.mult))
                    if step == 1:
                        link(nc.vector.tensor_scalar(whole[:, :], th[:, :], 1.0 / TWO_PI, ROUND, ALU.mult, ALU.add))
                        link(nc.vector.tensor_scalar(whole[:, :], whole[:, :], -ROUND, None, ALU.add))
                    if step in (2, 3, 4):
                        part = (PI_A, PI_B, PI_C)[step - 2]
                        link(nc.vector.scalar_tensor_tensor(th[:, :], whole[:, :], -part, th[:, :], ALU.mult, ALU.add))
                    if step == 5:
                        nc.vector.tensor_scalar(half[:, :], th[:, :], PI, -PI, ALU.min, ALU.max).then_inc(angles, 1)
                        link(nc.vector.tensor_scalar(whole[:, :], th[:, :], TWO_PI / 4, -TWO_PI, ALU.is_gt, ALU.mult))
                    if step == 6:
                        link(nc.vector.scalar_tensor_tensor(th[:, :], th[:, :], TWO_PI / 4, whole[:, :], ALU.add, ALU.add))
                        nc.vector.tensor_scalar(th[:, :], th[:, :], PI, -PI, ALU.min, ALU.max).then_inc(angles, 1)

                centre(0)
                for t in range(1, NCH):
                    centre(t)
                    turn_angles(t - 1)
                    invert(t - 1)
                    if t >= 2:
                        scale(t - 2)
                scale(NCH - 2)
                invert(NCH - 1)
                scale(NCH - 1)


def qkv_conv_rotary(nc, w_qkv, taps, cos_d, sin_d, qk_d, v_d, xn, k_sb):
    QK, TILES = 2 * CC, 3 * CC
    with ExitStack() as ctx:
        sb = lambda n, s, d=fp32: ctx.enter_context(nc.sbuf_tensor(n, s, d))
        sem = lambda n: ctx.enter_context(nc.semaphore("b_" + n))
        wt = [sb(f"wt{s}", [P, CC, P]) for s in range(2)]
        tp = [sb(f"tp{s}", [P, TAPS + 1]) for s in range(2)]
        raw = [sb(f"raw{s}", [P, PAD, PAD]) for s in range(2)]
        acc = [sb(f"acc{s}", [P, IMG, IMG]) for s in range(2)]
        cs = sb("cs", [P, N])
        sn = sb("sn", [P, N])
        crossed = sb("crossed", [P, N])
        rot = sb("rot", [P, N])
        ps_q = [ctx.enter_context(nc.psum_tensor(f"ps_q{b}", [P, CH], fp32)) for b in range(4)]
        ps_r = [ctx.enter_context(nc.psum_tensor(f"ps_r{b}", [P, CH], fp32)) for b in range(4)]
        w_in = [sem(f"w_in{s}") for s in range(2)]
        cs_in, borders, product_done, raw_done, centre_done, conv_step, conv_done = [
            sem(n) for n in ("cs_in", "borders", "product_done", "raw_done", "centre_done", "conv_step", "conv_done")]
        partner_done, partner_copied, direct_done, rotated, qk_out = [
            sem(n) for n in ("partner_done", "partner_copied", "direct_done", "rotated", "qk_out")]
        v_turned, v_copied, still, crossed_done = [sem(n) for n in ("v_turned", "v_copied", "still", "crossed_done")]
        v_out = [sem(f"v_out{s}") for s in range(2)]
        flat = [a[:, :, :].rearrange("p r c -> p (r c)") for a in acc]
        rows = CH // IMG

        with nc.Block() as block:
            @block.sync
            def _(sp):
                def load_tile(i, s):
                    wait(sp, product_done, NCH * (i - 1))
                    wait(sp, conv_done, i - 1)
                    i0 = bass.ds(i, 1)
                    sp.dma_start(wt[s][:, :, :], w_qkv[i0, :, :, :].rearrange("a p c o -> (a p) c o")).then_inc(w_in[s], 16)
                    sp.dma_start(tp[s][:, :], taps[i0, :, :].rearrange("a p t -> (a p) t")).then_inc(w_in[s], 16)

                def load_angles(hp):
                    wait(sp, rotated, 2 * hp)
                    for d, t in ((cs, cos_d), (sn, sin_d)):
                        for a in range(2):
                            src = t[bass.ds(hp * (2 * RH) + a * RH, RH), :]
                            for g in range(2):
                                at = a * HD + g * RH
                                sp.dma_start(d[at:at + RH, :], src).then_inc(cs_in, 16)

                load_tile(0, 0)
                load_tile(1, 1)
                sp.wait_ge(still, 2)

                def turn(hp):
                    load_angles(hp)
                    for s in range(2):
                        i = 2 * hp + s
                        load_tile(i + 2, s)
                        sp.wait_ge(rotated, i + 1)
                        sp.dma_start(qk_d[bass.ds(i, 1), :, :].rearrange("a p n -> (a p) n"), rot[:, :]).then_inc(qk_out, 16)

                turns(sp, CC, turn)
                for g in range(CC):
                    if g < 2:
                        load_tile(QK + 2 + g, g)
                    sp.wait_ge(v_copied, NCH * (g + 1))
                    dst = v_d.rearrange("(t p) c -> p t c", p=P)[:, :, g * P:(g + 1) * P]
                    sp.dma_start(dst, (rot if g % 2 == 0 else crossed)[:, :].rearrange("p (t c) -> p t c", c=P)).then_inc(v_out[g % 2], 16)
                sp.wait_ge(qk_out, 16 * QK)
                for s in range(2):
                    sp.wait_ge(v_out[s], 16 * (CC // 2))

            @block.tensor
            def _(pe):
                def products(i, s, loads):
                    pe.wait_ge(w_in[s], 32 * loads)
                    for n in range(NCH):
                        wait(pe, centre_done, NCH * i + n - 3)
                        for c in range(CC):
                            last = nc.tensor.matmul(ps_q[n % 4][:, :], wt[s][:, c, :], xn[:, c, n * CH:(n + 1) * CH], start=c == 0, stop=c == CC - 1)
                        last.then_inc(product_done, 1)

                def partners(i, s):
                    pe.wait_ge(conv_done, i + 1)
                    for n in range(NCH):
                        wait(pe, partner_copied, NCH * i + max(n - 3, 0))
                        nc.tensor.matmul(ps_r[n % 4][:, :], k_sb[:, K_ROT:K_ROT + P], flat[s][:, n * CH:(n + 1) * CH],
                                         start=True, stop=True).then_inc(partner_done, 1)

                def turn_values(g, s):
                    pe.wait_ge(conv_done, QK + g + 1)
                    if g == 0:
                        pe.wait_ge(partner_copied, NCH * QK)
                    for n in range(NCH):
                        wait(pe, v_copied, NCH * g + n - 3)
                        for b in range(4):
                            at = n * CH + b * P
                            last = nc.tensor.transpose(ps_r[n % 4][:, b * P:(b + 1) * P], flat[s][:, at:at + P], k_sb[:, K_ID:K_ID + P])
                        last.then_inc(v_turned, 1)

                products(0, 0, 1)

                def turn(hp):
                    products(2 * hp + 1, 1, hp + 1)
                    partners(2 * hp, 0)
                    products(2 * hp + 2, 0, hp + 2)
                    partners(2 * hp + 1, 1)

                turns(pe, CC, turn)
                for g in range(CC):
                    if g < CC - 1:
                        i = QK + g + 1
                        products(i, i % 2, i // 2 + 1)
                    turn_values(g, g % 2)

            @block.scalar
            def _(act):
                def copy_raw(i, s, loads):
                    act.wait_ge(w_in[s], 32 * loads)
                    wait(act, conv_done, i - 1)
                    if isinstance(i, int) and i - 2 >= QK:
                        act.wait_ge(v_turned, NCH * (i - 1 - QK))
                    else:
                        wait(act, direct_done, i - 1)
                        wait(act, partner_done, NCH * (i - 1))
                    mid = TAPS // 2
                    for n in range(NCH):
                        act.wait_ge(product_done, NCH * i + n + 1)
                        nc.scalar.activation(raw[s][:, 1 + n * rows:1 + (n + 1) * rows, 1:1 + IMG],
                                             ps_q[n % 4][:, :].rearrange("p (r c) -> p r c", c=IMG), ACT.Copy).then_inc(raw_done, 1)
                        nc.scalar.activation(flat[s][:, n * CH:(n + 1) * CH], ps_q[n % 4][:, :], ACT.Identity,
                                             bias=tp[s][:, TAPS:TAPS + 1], scale=tp[s][:, mid:mid + 1]).then_inc(centre_done, 1)

                def copy_partners(i):
                    wait(act, rotated, i)
                    for n in range(NCH):
                        act.wait_ge(partner_done, NCH * i + n + 1)
                        nc.scalar.activation(crossed[:, n * CH:(n + 1) * CH], ps_r[n % 4][:, :], ACT.Copy).then_inc(partner_copied, 1)

                def copy_values(g):
                    wait(act, v_out[g % 2], 16 * (g // 2))
                    if g == 0:
                        act.wait_ge(qk_out, 16 * QK)
                    if g == 1:
                        act.wait_ge(rotated, QK)
                    for n in range(NCH):
                        act.wait_ge(v_turned, NCH * g + n + 1)
                        nc.scalar.activation((rot if g % 2 == 0 else crossed)[:, n * CH:(n + 1) * CH], ps_r[n % 4][:, :], ACT.Copy).then_inc(v_copied, 1)

                act.wait_ge(borders, 8)
                copy_raw(0, 0, 1)

                def turn(hp):
                    for s in range(2):
                        copy_raw(2 * hp + s + 1, 1 - s, hp + s + 1)
                        copy_partners(2 * hp + s)

                turns(act, CC, turn)
                for g in range(CC):
                    if g < CC - 1:
                        copy_raw(QK + g + 1, (g + 1) % 2, (QK + g + 1) // 2 + 1)
                    copy_values(g)

            @block.vector
            def _(dve):
                def convolve(i, s, loads):
                    dve.wait_ge(w_in[s], 32 * loads)
                    dve.wait_ge(raw_done, NCH * (i + 1))
                    dve.wait_ge(centre_done, NCH * (i + 1))
                    others = [t for t in range(TAPS) if t != TAPS // 2]
                    for m, t in enumerate(others):
                        if m > 0:
                            dve.wait_ge(conv_step, (TAPS - 2) * i + m)
                        dy, dx = divmod(t, 3)
                        nc.vector.scalar_tensor_tensor(acc[s][:, :, :], raw[s][:, dy:dy + IMG, dx:dx + IMG], tp[s][:, t:t + 1], acc[s][:, :, :],
                                                       ALU.mult, ALU.add).then_inc(conv_done if t == others[-1] else conv_step, 1)

                for s in range(2):
                    for edge in (0, PAD - 1):
                        nc.vector.memset(raw[s][:, edge, :], 0.0).then_inc(borders, 1)
                        nc.vector.memset(raw[s][:, 1:1 + IMG, edge:edge + 1], 0.0).then_inc(borders, 1)

                def turn(hp):
                    for s in range(2):
                        convolve(2 * hp + s, s, hp + 1)

                dve.wait_ge(borders, 8)
                turns(dve, CC, turn)
                for g in range(CC):
                    convolve(QK + g, g % 2, QK // 2 + g // 2 + 1)

            @block.gpsimd
            def _(pool):
                nc.gpsimd.memset(cs[:, :], 1.0).then_inc(still, 1)
                nc.gpsimd.memset(sn[:, :], 0.0).then_inc(still, 1)

                def turn(hp):
                    pool.wait_ge(cs_in, 128 * (hp + 1))
                    for s in range(2):
                        i = 2 * hp + s
                        pool.wait_ge(conv_done, i + 1)
                        wait(pool, qk_out, 16 * i)
                        nc.gpsimd.tensor_tensor(rot[:, :], flat[s], cs[:, :], ALU.mult).then_inc(direct_done, 1)
                        pool.wait_ge(partner_copied, NCH * (i + 1))
                        nc.gpsimd.tensor_tensor(crossed[:, :], crossed[:, :], sn[:, :], ALU.mult).then_inc(crossed_done, 1)
                        pool.wait_ge(direct_done, i + 1)
                        pool.wait_ge(crossed_done, i + 1)
                        nc.gpsimd.tensor_tensor(rot[:, :], rot[:, :], crossed[:, :], ALU.add).then_inc(rotated, 1)

                turns(pool, CC, turn)


def attention_and_routing(nc, x_tok, masks, w_out, b_out, router_w, router_b, qk_d, v_d, x1_d, tn_d, ids_d,
                          k_sb, gates, experts_of, slots_of, starts, blocks):
    qv = qk_d.rearrange("(h t) p n -> t p h n", t=2)
    xt_v, x1_v, tn_v = (a.rearrange("(t p) c -> t p c", p=P) for a in (x_tok, x1_d, tn_d))
    one_tile = lambda a, t: a[bass.ds(t, 1), :, :].rearrange("a p n -> (a p) n")
    KC = WIN // P
    PAIR = 2 * NH
    PAIRS = NT // 2
    AHEAD, BEHIND = 3, 2
    SB = 2
    with ExitStack() as ctx:
        sb = lambda n, s, d=fp32: ctx.enter_context(nc.sbuf_tensor(n, s, d))
        sem = lambda n: ctx.enter_context(nc.semaphore("c_" + n))
        ps = lambda n: ctx.enter_context(nc.psum_tensor(n, [P, CH], fp32))
        q = [sb(f"q{s}", [P, CC, P]) for s in range(2)]
        k = [sb(f"k{s}", [P, CC, WIN]) for s in range(2)]
        v = [sb(f"v{s}", [P, KC, C]) for s in range(2)]
        mask = sb("mask", [P, 3, WIN])
        xt = [sb(f"xt{s}", [P, C]) for s in range(2)]
        score = [sb(f"score{b}", [P, WIN]) for b in range(4)]
        prob = [sb(f"prob{b}", [P, WIN]) for b in range(4)]
        probT = [sb(f"probT{b}", [P, WIN]) for b in range(4)]
        top, ntop = sb("top", [P, 4]), sb("ntop", [P, 4])
        total = [sb(f"total{s}", [P, NH]) for s in range(2)]
        inv = sb("inv", [P, NH])
        ao, aoT = sb("ao", [P, C]), sb("aoT", [P, C])
        x1 = [sb(f"x1{s}", [P, C]) for s in range(2)]
        tn = [sb(f"tn{s}", [P, C]) for s in range(2)]
        tnT = sb("tnT", [P, C])
        stats, moments = sb("stats", [P, 6]), sb("moments", [P, 2])
        var_eps, power, rstd = sb("var_eps", [P, 1]), sb("power", [P, 1]), sb("rstd", [P, 1])
        wo, bo, bo_all = sb("wo", [P, CC, C]), sb("bo", [1, C]), sb("bo_all", [P, C])
        rw, rb = sb("rw", [P, CC, E]), sb("rb", [1, E])
        ones = sb("ones", [P, P])
        logit, expo = sb("logit", [P, E]), sb("expo", [P, E])
        big8, index8, index_f = sb("big8", [P, 8]), sb("index8", [P, 8], u32), sb("index_f", [P, TOPK])
        nbig, esum, gsum = sb("nbig", [P, 1]), sb("esum", [P, 1]), sb("gsum", [P, 1])
        chosen, picked = sb("chosen", [P, TOPK, E]), sb("picked", [P, TOPK, E])
        taken, counts, rank = sb("taken", [P, E]), sb("counts", [P, E]), sb("rank", [P, E])
        slot, fits, row, gate6, away = [sb(n, [P, TOPK]) for n in ("slot", "fits", "row", "gate6", "away")]
        row_to = [sb(f"row_to{s}", [P, TOPK], i32) for s in range(2)]
        token_f = sb("token_f", [P, 1])
        token = [sb(f"token{s}", [P, 1], i32) for s in range(2)]
        zeros = sb("zeros", [P, SLOTS // P], i32)
        n_blocks, n_blocksT, ends = sb("n_blocks", [P, E]), sb("n_blocksT", [E, P]), sb("ends", [E, 1])
        ended = sb("ended", [E, NB])
        be_f, br_f, slot_f, turn_f = sb("be_f", [1, NB]), sb("br_f", [1, NB]), sb("slot_f", [1, NB]), sb("turn_f", [1, 1])
        ps_s = [ps(f"ps_s{b}") for b in range(SB)]
        ps_t = [ps(f"ps_t{b}") for b in range(2)]
        ps_o = [ps(f"ps_o{b}") for b in range(2)]
        ps_x, ps_r = ps("ps_x"), ps("ps_r")

        tile_in, xt_in, x1_out, tn_out, ids_out = [
            [sem(f"{n}{s}") for s in range(2)] for n in ("tile_in", "xt_in", "x1_out", "tn_out", "ids_out")]
        w_in, setup, zeroed = sem("w_in"), sem("setup"), sem("zeroed")
        scored, masked, ntop_done, exp_done, turned, value_done, heads_done = [
            sem(n) for n in ("scored", "masked", "ntop_done", "exp_done", "turned", "value_done", "heads_done")]
        aoT_done, aoT_copied, projected, x1_done, var_done, rstd_done, tn_done, tnT_done, tnT_copied = [
            sem(n) for n in ("aoT_done", "aoT_copied", "projected", "x1_done", "var_done", "rstd_done", "tn_done", "tnT_done", "tnT_copied")]
        logits_done, nbig_done, routed_exp, taken_done, ranked, rows_done, steps = [
            sem(n) for n in ("logits_done", "nbig_done", "routed_exp", "taken_done", "ranked", "rows_done", "dve_steps")]
        turn_copied = [sem(f"turn_copied{b}") for b in range(2)]
        logits_read, bias_spread, bias_copied, bias_added = [sem(n) for n in ("logits_read", "bias_spread", "bias_copied", "bias_added")]
        passed, passed_pool = sem("passed"), sem("passed_pool")
        blocks_done, map_step, map_done = sem("blocks_done"), sem("map_step"), sem("map_done")

        with nc.Block() as block:
            @block.sync
            def _(sp):
                def load_tile(t, s, first):
                    wait(sp, value_done, NH * (t - 1))
                    sp.dma_start(q[s][:, :, :], qv[0][:, :, bass.ds(t * P, P)]).then_inc(tile_in[s], 16)
                    sp.dma_start(k[s][:, :, :], qv[1][:, :, bass.ds(first, WIN)]).then_inc(tile_in[s], 16)
                    sp.dma_start(v[s][:, :, :], v_d[bass.ds(first, WIN), :].rearrange("(c p) n -> p c n", p=P)).then_inc(tile_in[s], 16)
                    wait(sp, x1_done, t - 1)
                    sp.dma_start(xt[s][:, :], one_tile(xt_v, t)).then_inc(xt_in[s], 16)

                load_tile(0, 0, 0)
                for d, src in ((mask[:, :, :], masks.rearrange("m p n -> p m n")), (wo[:, :, :], w_out), (bo[:, :], b_out),
                               (rw[:, :, :], router_w), (rb[:, :], router_b)):
                    sp.dma_start(d, src).then_inc(w_in, 16)
                load_tile(1, 1, 0)
                sp.wait_ge(setup, 5)
                sp.dma_start(ids_d.rearrange("(p n) a -> p (n a)", p=P), zeros[:, :]).then_inc(zeroed, 16)
                for t in range(2, 4):
                    load_tile(t, t % 2, t * P - KW // 2 * IMG)
                with sp.Fori(2, PAIRS - 1) as j:
                    for s in range(2):
                        load_tile(2 * j + s, s, j * (2 * P) + (s * P - KW // 2 * IMG))
                for t in range(NT - 2, NT):
                    load_tile(t, t % 2, N - WIN)
                sp.wait_ge(map_done, 1)

            TAIL = 16

            def tiles(eng, body, tail):
                body(0)
                body(1)
                with eng.Fori(2, PAIRS - 2) as j:
                    body(j)
                body(PAIRS - 2)
                body(PAIRS - 1)
                for step in range(TAIL):
                    tail(NT - 1, 1, PAIRS - 1, step)
                    if step + NH < TAIL:
                        tail(NT - 2, 0, PAIRS - 1, step + NH)

            def tail_between(j, i, tail):
                t, step = i // NH - 1, i % NH
                for back, at in ((0, step), (1, step + NH)):
                    tile = t - back
                    if at < TAIL and not (isinstance(j, int) and 2 * j + tile < 0):
                        tail(2 * j + tile, tile % 2, j + tile // 2, at)

            def is_last(j):
                return isinstance(j, int) and j == PAIRS - 1

            @block.tensor
            def _(pe):
                ident = k_sb[:, K_ID:K_ID + P]

                def score_head(j, i):
                    s, h = i // NH % 2, i % NH
                    if h == 0:
                        pe.wait_ge(tile_in[s], 48 * (j + (1 if i < PAIR else 2)))
                    wait(pe, masked, PAIR * j + i - 1)
                    a = h % 2 * HD
                    nc.tensor.matmul(ps_s[h % SB][:, :], q[s][a:a + HD, h // 2, :], k[s][a:a + HD, h // 2, :],
                                     start=True, stop=True).then_inc(scored, 1)

                def turn_head(j, i):
                    pe.wait_ge(exp_done, PAIR * j + i + 1)
                    wait(pe, turn_copied[i % 2], NH * j + i // 2)
                    for c in range(KC):
                        at = slice(c * P, (c + 1) * P)
                        last = nc.tensor.transpose(ps_t[i % 2][:, at], prob[i % 4][:, at], ident)
                    last.then_inc(turned, 1)

                def value_head(j, i):
                    s, h = i // NH % 2, i % NH
                    pe.wait_ge(turn_copied[i % 2], NH * j + i // 2 + 1)
                    if h == 0:
                        wait(pe, heads_done, 2 * j + i // NH)
                    for c in range(KC):
                        last = nc.tensor.matmul(ps_o[h % 2][:, h // 2 * P:(h // 2 + 1) * P], probT[i % 4][:, c * P:(c + 1) * P],
                                                v[s][:, c, h // 2 * P:(h // 2 + 1) * P], start=c == 0, stop=c == KC - 1)
                    last.then_inc(value_done, 1)

                def turn_tile(src, done):
                    for c in range(CC):
                        at = slice(c * P, (c + 1) * P)
                        last = nc.tensor.transpose(ps_x[:, at], src[:, at], ident)
                    last.then_inc(done, 1)

                def tail(t, s, uses, step):
                    if step == 2:
                        pe.wait_ge(heads_done, t + 1)
                        wait(pe, logits_read, t)
                        turn_tile(ao, aoT_done)
                    if step == 3:
                        pe.wait_ge(aoT_copied, t + 1)
                        for c in range(CC):
                            last = nc.tensor.matmul(ps_x[:, :], aoT[:, c * P:(c + 1) * P], wo[:, c, :], start=c == 0, stop=c == CC - 1)
                        last.then_inc(projected, 1)
                    if step == 5:
                        pe.wait_ge(tn_done, t + 1)
                        turn_tile(tn[s], tnT_done)
                    if step == 6:
                        pe.wait_ge(tnT_copied, t + 1)
                        nc.tensor.matmul(ps_x[:, 0:E], ones[0:1, :], rb[:, :], start=True, stop=False)
                        for c in range(CC):
                            last = nc.tensor.matmul(ps_x[:, 0:E], tnT[:, c * P:(c + 1) * P], rw[:, c, :], start=False, stop=c == CC - 1)
                        last.then_inc(logits_done, 1)
                    if step == 11:
                        pe.wait_ge(taken_done, t + 1)
                        wait(pe, rows_done, t)
                        if isinstance(t, int) and t == 0:
                            pe.wait_ge(bias_copied, 1)
                        nc.tensor.matmul(ps_r[:, 0:E], k_sb[:, K_BEFORE:K_BEFORE + P], taken[:, :], start=True, stop=True)
                        nc.tensor.matmul(ps_r[:, E:2 * E], ones[:, :], taken[:, :], start=True, stop=True).then_inc(ranked, 1)

                def body(j):
                    for i in range(PAIR):
                        if not (is_last(j) and i + AHEAD >= PAIR):
                            score_head(j, i + AHEAD)
                        turn_head(j, i)
                        if i >= BEHIND or not (isinstance(j, int) and j == 0):
                            value_head(j, i - BEHIND)
                        tail_between(j, i, tail)
                    if is_last(j):
                        for i in range(PAIR - BEHIND, PAIR):
                            value_head(j, i)

                pe.wait_ge(w_in, 80)
                pe.wait_ge(setup, 5)
                nc.tensor.matmul(ps_r[:, :], ones[0:1, :], bo[:, :], start=True, stop=True).then_inc(bias_spread, 1)
                for i in range(AHEAD):
                    score_head(0, i)
                tiles(pe, body, tail)
                pe.wait_ge(blocks_done, 1)
                nc.tensor.transpose(ps_x[0:E, 0:P], n_blocks[:, :], ident).then_inc(map_step, 1)
                pe.wait_ge(blocks_done, 2)
                nc.tensor.matmul(ps_x[0:E, P:P + 1], k_sb[0:E, K_UPTO:K_UPTO + E], n_blocksT[:, 0:1], start=True, stop=True).then_inc(map_step, 1)
                nc.tensor.matmul(ps_x[:, 2 * P:2 * P + E], n_blocksT[:, :], k_sb[0:E, K_BEFORE:K_BEFORE + E], start=True, stop=True).then_inc(map_step, 1)
                pe.wait_ge(blocks_done, 3)
                nc.tensor.matmul(ps_o[0][0:1, 0:NB], ones[0:E, 0:1], ended[:, :], start=True, stop=True)
                nc.tensor.matmul(ps_t[0][0:1, 0:NB], n_blocksT[:, 0:1], ended[:, :], start=True, stop=True).then_inc(map_step, 1)

            @block.scalar
            def _(act):
                def exp_head(j, i):
                    s, h = i // NH % 2, i % NH
                    act.wait_ge(ntop_done, PAIR * j + i + 1)
                    wait(act, turned, PAIR * j + i - 3)
                    if h == 0:
                        wait(act, heads_done, 2 * j + i // NH - 1)
                    nc.scalar.activation(prob[i % 4][:, :], score[i % 4][:, :], ACT.Exp, bias=ntop[:, i % 4:i % 4 + 1], scale=SCALE,
                                         accum_out=total[s][:, h:h + 1]).then_inc(exp_done, 1)

                def tail(t, s, uses, step):
                    if step == 3:
                        act.wait_ge(aoT_done, t + 1)
                        nc.scalar.activation(aoT[:, :], ps_x[:, :], ACT.Copy).then_inc(aoT_copied, 1)
                    if step == 5:
                        act.wait_ge(x1_done, t + 1)
                        act.dma_start(one_tile(x1_v, t), x1[s][:, :]).then_inc(x1_out[s], 16)
                    if step == 6:
                        act.wait_ge(tn_done, t + 1)
                        act.dma_start(one_tile(tn_v, t), tn[s][:, :]).then_inc(tn_out[s], 16)
                    if step == 6:
                        act.wait_ge(tnT_done, t + 1)
                        nc.scalar.activation(tnT[:, :], ps_x[:, :], ACT.Copy).then_inc(tnT_copied, 1)
                    if step == 8:
                        act.wait_ge(nbig_done, t + 1)
                        nc.scalar.activation(expo[:, :], logit[:, :], ACT.Exp, bias=nbig[:, :], accum_out=esum[:, :]).then_inc(routed_exp, 1)

                def body(j):
                    for i in range(PAIR):
                        tail_between(j, i, tail)
                        if i % 2 == 1:
                            act.wait_ge(turned, PAIR * j + i + 1)
                            nc.scalar.activation(probT[i % 4][:, :], ps_t[1][:, :], ACT.Copy).then_inc(turn_copied[1], 1)
                        if not (is_last(j) and i + AHEAD >= PAIR):
                            exp_head(j, i + AHEAD)

                for i in range(AHEAD):
                    exp_head(0, i)
                tiles(act, body, tail)
                for s in range(2):
                    act.wait_ge(x1_out[s], 16 * PAIRS)
                    act.wait_ge(tn_out[s], 16 * PAIRS)

            @block.vector
            def _(dve):
                link = Chain(dve, steps)
                wide = lambda a: a.unsqueeze(2).to_broadcast([P, TOPK, E])

                def mask_head(j, i):
                    edge = isinstance(j, int)
                    t = 2 * j + i // NH if edge else None
                    kind = 1 if t is None or 2 <= t < NT - 2 else 0 if t < 2 else 2
                    dve.wait_ge(scored, PAIR * j + i + 1)
                    wait(dve, exp_done, PAIR * j + i - 3)
                    settled(dve, passed)
                    b = i % 4
                    nc.vector.tensor_tensor_reduce(score[b][:, :], ps_s[i % NH % SB][:, :], mask[:, kind, :], 1.0, -3e38, ALU.add, ALU.max,
                                                   top[:, b:b + 1]).then_inc(masked, 1)
                    dve.wait_ge(masked, PAIR * j + i + 1)
                    nc.vector.tensor_scalar(ntop[:, b:b + 1], top[:, b:b + 1], -SCALE, None, ALU.mult).then_inc(ntop_done, 1)

                def tail(t, s, uses, step):
                    if step == 2:
                        dve.wait_ge(value_done, NH * (t + 1))
                        wait(dve, aoT_done, t)
                        link(nc.vector.reciprocal(inv[:, :], total[s][:, :]))
                        for b in range(2):
                            half = lambda a: a[:, :].rearrange("p (h b d) -> p h b d", b=2, d=HD)[:, :, b, :]
                            last = nc.vector.tensor_tensor(half(ao), half(ps_o[b]), inv[:, :].rearrange("p (h b) -> p h b", b=2)[:, :, b].unsqueeze(2)
                                                           .to_broadcast([P, NH // 2, HD]), ALU.mult)
                        last.then_inc(heads_done, 1)
                    if step == 4:
                        dve.wait_ge(projected, t + 1)
                        dve.wait_ge(bias_added, t + 1)
                        wait(dve, x1_out[s], 16 * uses)
                        nc.vector.tensor_tensor(x1[s][:, :], ps_x[:, :], xt[s][:, :], ALU.add).then_inc(x1_done, 1)
                        dve.wait_ge(x1_done, t + 1)
                        link(nc.vector.bn_stats(stats[:, :], x1[s][:, :]), passed)
                        link(nc.vector.bn_aggr(moments[:, :], stats[:, :]))
                        nc.vector.tensor_scalar(var_eps[:, :], moments[:, 1:2], EPS2, None, ALU.add).then_inc(var_done, 1)
                    if step == 5:
                        dve.wait_ge(rstd_done, t + 1)
                        wait(dve, tn_out[s], 16 * uses)
                        nc.vector.tensor_scalar(tn[s][:, :], x1[s][:, :], moments[:, 0:1], rstd[:, :], ALU.subtract, ALU.mult).then_inc(tn_done, 1)
                    if step == 7:
                        dve.wait_ge(logits_done, t + 1)
                        nc.vector.tensor_copy(logit[:, :], ps_x[:, 0:E]).then_inc(logits_read, 1)
                        dve.wait_ge(logits_read, t + 1)
                        settled(dve, passed)
                        link(nc.vector.max(big8[:, :], logit[:, :]))
                        nc.vector.tensor_scalar(nbig[:, :], big8[:, 0:1], -1.0, None, ALU.mult).then_inc(nbig_done, 1)
                    if step == 9:
                        dve.wait_ge(routed_exp, t + 1)
                        link(nc.vector.reciprocal(esum[:, :], esum[:, :]))
                        link(nc.vector.tensor_scalar(expo[:, :], expo[:, :], esum[:, :], None, ALU.mult), passed)
                        link(nc.vector.max(big8[:, :], expo[:, :]), passed)
                        link(nc.vector.max_index(index8[:, :], big8[:, :], expo[:, :]))
                        link(nc.vector.tensor_copy(index_f[:, :], index8[:, 0:TOPK]))
                    if step == 10:
                        link(nc.vector.tensor_tensor(chosen[:, :, :], k_sb[:, K_IOTA:K_IOTA + E].unsqueeze(1).to_broadcast([P, TOPK, E]),
                                                     wide(index_f[:, :]), ALU.is_equal))
                        nc.vector.tensor_reduce(taken[:, :], chosen[:, :, :].rearrange("p k e -> p e k"), AX.X, ALU.add).then_inc(taken_done, 1)
                    if step == 11:
                        link(nc.vector.tensor_reduce(gsum[:, :], big8[:, 0:TOPK], AX.X, ALU.add))
                        link(nc.vector.tensor_scalar(gsum[:, :], gsum[:, :], 1e-9, None, ALU.add))
                        link(nc.vector.reciprocal(gsum[:, :], gsum[:, :]))
                        link(nc.vector.tensor_scalar(gate6[:, :], big8[:, 0:TOPK], gsum[:, :], None, ALU.mult))
                    if step == 13:
                        dve.wait_ge(ranked, t + 1)
                        link(nc.vector.tensor_tensor(rank[:, :], ps_r[:, 0:E], counts[:, :], ALU.add))
                        link(nc.vector.tensor_tensor(counts[:, :], counts[:, :], ps_r[:, E:2 * E], ALU.add))
                        link(nc.vector.tensor_tensor(picked[:, :, :], chosen[:, :, :], rank[:, :].unsqueeze(1).to_broadcast([P, TOPK, E]), ALU.mult))
                    if step == 14:
                        link(nc.vector.tensor_reduce(slot[:, :], picked[:, :, :], AX.X, ALU.add))
                        link(nc.vector.tensor_scalar(fits[:, :], slot[:, :], float(CAP), None, ALU.is_lt))
                        link(nc.vector.scalar_tensor_tensor(row[:, :], index_f[:, :], float(CAP), slot[:, :], ALU.mult, ALU.add))
                        nc.vector.tensor_tensor(gates[:, bass.ds(t * TOPK, TOPK)], gate6[:, :], fits[:, :], ALU.mult)
                    if step == 15:
                        wait(dve, ids_out[s], 16 * TOPK * uses)
                        nc.vector.tensor_copy(experts_of[:, bass.ds(t * TOPK, TOPK)], index_f[:, :])
                        nc.vector.tensor_copy(slots_of[:, bass.ds(t * TOPK, TOPK)], slot[:, :])
                        link(nc.vector.tensor_scalar(away[:, :], fits[:, :], -FAR, FAR, ALU.mult, ALU.add))
                        link(nc.vector.tensor_tensor(row_to[s][:, :], row[:, :], away[:, :], ALU.add))
                        link(nc.vector.tensor_copy(token[s][:, :], token_f[:, :]))
                        nc.vector.tensor_scalar(token_f[:, :], token_f[:, :], float(P), None, ALU.add).then_inc(rows_done, 1)
                        dve.wait_ge(rows_done, t + 1)

                def body(j):
                    for i in range(PAIR):
                        tail_between(j, i, tail)
                        if not (is_last(j) and i + AHEAD >= PAIR):
                            mask_head(j, i + AHEAD)
                        if i % 2 == 0:
                            dve.wait_ge(turned, PAIR * j + i + 1)
                            nc.vector.tensor_copy(probT[i % 4][:, :], ps_t[0][:, :]).then_inc(turn_copied[0], 1)

                def looped_body(j):
                    if isinstance(j, int):
                        return body(j)
                    link.enter(j - 1, 2 * TAIL_STEPS)
                    body(j)
                    link.leave(j, PAIRS - 4)

                TAIL_STEPS = 23
                nc.vector.memset(ones[:, :], 1.0).then_inc(setup, 1)
                nc.vector.memset(zeros[:, :], 0).then_inc(setup, 1)
                nc.vector.memset(power[:, :], -0.5).then_inc(setup, 1)
                nc.vector.memset(counts[:, :], 0.0).then_inc(setup, 1)
                nc.vector.tensor_copy(token_f[:, :], k_sb[:, K_P:K_P + 1]).then_inc(setup, 1)
                dve.wait_ge(setup, 5)
                dve.wait_ge(w_in, 80)
                dve.wait_ge(bias_spread, 1)
                nc.vector.tensor_copy(bo_all[:, :], ps_r[:, :]).then_inc(bias_copied, 1)
                for i in range(AHEAD):
                    mask_head(0, i)
                tiles(dve, looped_body, tail)

                link(nc.vector.tensor_scalar(n_blocks[:, :], counts[:, :], 0.0, None, ALU.is_gt))
                for m in range(1, CAP // P - 1):
                    link(nc.vector.scalar_tensor_tensor(n_blocks[:, :], counts[:, :], float(m * P), n_blocks[:, :], ALU.is_gt, ALU.add))
                nc.vector.scalar_tensor_tensor(n_blocks[:, :], counts[:, :], float(CAP - P), n_blocks[:, :], ALU.is_gt, ALU.add).then_inc(blocks_done, 1)
                dve.wait_ge(map_step, 1)
                nc.vector.tensor_copy(n_blocksT[:, :], ps_x[0:E, 0:P]).then_inc(blocks_done, 1)
                dve.wait_ge(map_step, 3)
                nc.vector.tensor_scalar(starts[:, :], ps_x[:, 2 * P:2 * P + E], float(P), None, ALU.mult)
                link(nc.vector.tensor_copy(ends[:, :], ps_x[0:E, P:P + 1]))
                nc.vector.tensor_scalar(ended[:, :], k_sb[0:E, K_IOTA:K_IOTA + NB], ends[:, :], None, ALU.is_ge).then_inc(blocks_done, 1)
                link(nc.vector.tensor_scalar(blocks.first[:, :], ps_x[0:1, 2 * P:2 * P + E], 1.0, None, ALU.add))
                link(nc.vector.tensor_tensor(turn_f[:, :], ps_x[0:1, 2 * P + E - 1:2 * P + E], n_blocks[0:1, E - 1:E], ALU.add))
                link(nc.vector.tensor_scalar(turn_f[:, :], turn_f[:, :], 1.0 / TURN, -1.0 / TURN - ROUND_DOWN, ALU.mult, ALU.add))
                link(nc.vector.tensor_scalar(turn_f[:, :], turn_f[:, :], ROUND, None, ALU.add))
                link(nc.vector.tensor_scalar(blocks.later_turns[:, :], turn_f[:, :], -ROUND - 1.0, 0.0, ALU.add, ALU.max))
                dve.wait_ge(map_step, 4)
                link(nc.vector.tensor_scalar(be_f[:, :], ps_o[0][0:1, 0:NB], float(E - 1), None, ALU.min))
                link(nc.vector.tensor_copy(blocks.expert[:, :], be_f[:, :]))
                link(nc.vector.tensor_scalar(slot_f[:, :], be_f[:, :], 1.0 / W_SLOTS, -ROUND_DOWN, ALU.mult, ALU.add))
                link(nc.vector.tensor_scalar(slot_f[:, :], slot_f[:, :], ROUND, None, ALU.add))
                link(nc.vector.tensor_scalar(slot_f[:, :], slot_f[:, :], -ROUND, None, ALU.add))
                link(nc.vector.scalar_tensor_tensor(blocks.slot[:, :], slot_f[:, :], -float(W_SLOTS), be_f[:, :], ALU.mult, ALU.add))
                link(nc.vector.tensor_tensor(br_f[:, :], k_sb[0:1, K_IOTA:K_IOTA + NB], ps_t[0][0:1, 0:NB], ALU.subtract))
                link(nc.vector.tensor_scalar(br_f[:, :], br_f[:, :], float(P), None, ALU.mult))
                nc.vector.scalar_tensor_tensor(blocks.row[:, :], ps_o[0][0:1, 0:NB], float(CAP), br_f[:, :], ALU.mult, ALU.add).then_inc(map_done, 1)

            @block.gpsimd
            def _(pool):
                def add_bias(t, s, uses):
                    pool.wait_ge(xt_in[s], 16 * (uses + 1))
                    nc.gpsimd.tensor_tensor(xt[s][:, :], xt[s][:, :], bo_all[:, :], ALU.add).then_inc(bias_added, 1)

                def power_half(t):
                    pool.wait_ge(var_done, t + 1)
                    nc.gpsimd.tensor_tensor(rstd[:, :], var_eps[:, :], power[:, :], ALU.pow).then_inc(rstd_done, 1)

                def send_ids(t, s):
                    pool.wait_ge(rows_done, t + 1)
                    settled(pool, passed_pool)
                    for c in range(TOPK):
                        nc.gpsimd.indirect_dma_start(out=ids_d, out_offset=bass.IndirectOffsetOnAxis(row_to[s][:, c:c + 1], 0),
                                                     in_=token[s][:, :], in_offset=None, bounds_check=E * CAP - 1,
                                                     oob_is_err=False).then_inc(ids_out[s], 16)

                pool.wait_ge(setup, 5)
                pool.wait_ge(zeroed, 16)
                pool.wait_ge(bias_copied, 1)
                add_bias(0, 0, 0)
                power_half(0)

                def turn(j):
                    for s in range(2):
                        add_bias(2 * j + s + 1, 1 - s, j + s)
                        power_half(2 * j + s + 1)
                        send_ids(2 * j + s, s)

                turns(pool, PAIRS - 1, turn)
                add_bias(NT - 1, 1, PAIRS - 1)
                power_half(NT - 1)
                for s in range(2):
                    send_ids(NT - 2 + s, s)
                for s in range(2):
                    pool.wait_ge(ids_out[s], 16 * TOPK * PAIRS)


class Blocks:

    def __init__(self, sb):
        self.expert = sb("block_expert", [1, NB], i32)
        self.slot = sb("block_slot", [1, NB], i32)
        self.row = sb("block_row", [1, NB], i32)
        self.first = sb("expert_first", [1, E], i32)
        self.later_turns = sb("later_turns", [1, 1], i32)


def pipeline(eng, width, count, first, step, last, link=None, links=0, last_turn=None):
    first()
    for s in range(1, width):
        step(0, s)
    with eng.Fori(1, count - 1) as j:
        if link is not None:
            link.enter(j, links)
        if last_turn is None:
            for s in range(width):
                step(j, s)
        else:
            with eng.If(j < last_turn):
                for s in range(width):
                    step(j, s)
        if link is not None:
            link.leave(j, count - 2)
    if last_turn is None:
        last_turn = count - 1
    for s in range(width - 1):
        step(last_turn, s)
    last(last_turn)


def expert_blocks(nc, experts, tn_d, ids_d, rows_d, k_sb, blocks, shared):
    UP, DOWN = CC * 2 * F, FC * C
    with ExitStack() as ctx:
        sb = lambda n, s, d=fp32: ctx.enter_context(nc.sbuf_tensor(n, s, d))
        sem = lambda n: ctx.enter_context(nc.semaphore("d_" + n))
        ps = lambda n: ctx.enter_context(nc.psum_tensor(n, [P, CH], fp32))
        w = sb("w", [P, W_SLOTS, UP + DOWN])
        zero = sb("zero", [P, C])
        ids = [sb(f"ids{s}", [P, 1], i32) for s in range(4)]
        xg = [sb(f"xg{s}", [P, C]) for s in range(4)]
        xT = [sb(f"xT{s}", [P, C]) for s in range(2)]
        sg = [sb(f"sg{s}", [P, F]) for s in range(2)]
        h = [sb(f"h{s}", [P, F]) for s in range(2)]
        hT = [sb(f"hT{s}", [P, F]) for s in range(2)]
        y = [sb(f"y{s}", [P, C]) for s in range(4)]
        ps_x, ps_u, ps_h, ps_y = [[ps(f"{n}{s}") for s in range(2)] for n in ("ps_x", "ps_u", "ps_h", "ps_y")]
        ids_in, x_in, y_out = [[sem(f"{n}{s}") for s in range(4)] for n in ("ids_in", "x_in", "y_out")]
        w_in, zero_set, cleared = sem("w_in"), sem("zero_set"), sem("cleared")
        shared_in = [sem(f"shared_in{n}") for n in range(len(shared))]
        x_turned, x_copied, up_done, silu_done, h_done, h_turned, h_copied, down_done, y_copied = [
            sem(n) for n in ("x_turned", "x_copied", "up_done", "silu_done", "h_done", "h_turned", "h_copied", "down_done", "y_copied")]
        passed, passed_pool, passed_act = sem("passed"), sem("passed_pool"), sem("passed_act")
        R = TURN
        TURNS = NB // R
        last_used = lambda eng: eng.value_load(blocks.later_turns[0:1, 0:1], min_val=0, max_val=TURNS - 2) + 1

        with nc.Block() as block:
            @block.sync
            def _(sp):
                def load(expert):
                    sp.dma_start(w[:, expert % W_SLOTS, :], experts[expert, :, :]).then_inc(w_in, 16)

                for expert in range(W_SLOTS):
                    wait(sp, w_in, 16 * expert)
                    load(expert)
                for n, (to, src) in enumerate(shared):
                    sp.dma_start(to[:, :, :], src).then_inc(shared_in[n], 16)
                with sp.Fori(1, E // W_SLOTS) as j:
                    for s in range(W_SLOTS):
                        first = sp.value_load(blocks.first[0:1, bass.ds(W_SLOTS * j + (s - W_SLOTS + 1), 1)], min_val=1, max_val=NB + 1)
                        sp.wait_ge(down_done, first)
                        settled(sp, passed)
                        sp.wait_ge(w_in, W_SLOTS * 16 * j + 16 * s)
                        settled(sp, passed)
                        sp.dma_start(w[:, s, :], experts[bass.ds(W_SLOTS * j + s, 1), :, :].rearrange("a p n -> (a p) n")).then_inc(w_in, 16)
                sp.wait_ge(zero_set, 1)
                last_turn = last_used(sp)
                with sp.Fori(1, TURNS) as j:
                    with sp.If(j > last_turn):
                        sp.dma_start(rows_d[bass.ds(j * (R * P), R * P), :].rearrange("(r p) n -> p r n", p=P),
                                     zero[:, :].unsqueeze(1).to_broadcast([P, R, C])).then_inc(cleared, 16)
                    with sp.Else():
                        sp.sem_inc(cleared, 16)
                    sp.wait_ge(cleared, 16 * j)
                    settled(sp, passed)
                for n in range(len(shared)):
                    sp.wait_ge(shared_in[n], 16)

            @block.gpsimd
            def _(pool):
                def load_ids(j, i):
                    s = i % R
                    row = pool.value_load(blocks.row[0:1, bass.ds(R * j + i, 1)], min_val=0, max_val=SLOTS - P)
                    wait(pool, x_in[s], 16 * (j + i // R))
                    settled(pool, passed_pool)
                    pool.dma_start(ids[s][:, :], ids_d[bass.ds(row, P), :]).then_inc(ids_in[s], 16)

                def fetch(j, s):
                    pool.wait_ge(ids_in[s], 16 * j + 16)
                    wait(pool, x_turned, R * j + s - R + 1)
                    settled(pool, passed_pool)
                    nc.gpsimd.indirect_dma_start(out=xg[s][:, :], out_offset=None, in_=tn_d,
                                                 in_offset=bass.IndirectOffsetOnAxis(ids[s][:, :], 0)).then_inc(x_in[s], 16)

                def step(j, s):
                    load_ids(j, s + 2)
                    fetch(j, s)

                last_turn = last_used(pool)
                load_ids(0, 0)
                load_ids(0, 1)
                for s in range(R):
                    step(0, s)
                with pool.Fori(1, TURNS - 1) as j:
                    with pool.If(j < last_turn):
                        for s in range(R):
                            step(j, s)
                for s in range(R):
                    if s < R - 2:
                        load_ids(last_turn, s + 2)
                    fetch(last_turn, s)

            @block.tensor
            def _(pe):
                ident = k_sb[:, K_ID:K_ID + P]

                def turn_x(j, i):
                    s = i % R
                    b = R * j + i
                    pe.wait_ge(x_in[s], 16 * (j + i // R + 1))
                    wait(pe, x_copied, b - 1)
                    for c in range(CC):
                        at = slice(c * P, (c + 1) * P)
                        last = nc.tensor.transpose(ps_x[i % 2][:, at], xg[s][:, at], ident)
                    last.then_inc(x_turned, 1)

                def slot_columns(slot, at, width):
                    return w[:, bass.ds(slot, 1), at:at + width].rearrange("p a n -> p (a n)")

                def weights(b):
                    return pe.value_load(blocks.slot[0:1, bass.ds(b, 1)], min_val=0, max_val=W_SLOTS - 1)

                def expert_of(b):
                    return pe.value_load(blocks.expert[0:1, bass.ds(b, 1)], min_val=0, max_val=E - 1)

                def up(j, s, expert, slot):
                    b = R * j + s
                    pe.wait_ge(x_copied, b + 1)
                    pe.wait_ge(w_in, 16 * expert + 16)
                    wait(pe, h_done, b - 1)
                    for c in range(CC):
                        last = nc.tensor.matmul(ps_u[s % 2][:, :], xT[s % 2][:, c * P:(c + 1) * P], slot_columns(slot, c * 2 * F, 2 * F),
                                                start=c == 0, stop=c == CC - 1)
                    last.then_inc(up_done, 1)

                def turn_h(j, i):
                    b = R * j + i
                    pe.wait_ge(h_done, b + 1)
                    wait(pe, h_copied, b - 1)
                    for c in range(FC):
                        at = slice(c * P, (c + 1) * P)
                        last = nc.tensor.transpose(ps_h[i % 2][:, at], h[i % 2][:, at], ident)
                    last.then_inc(h_turned, 1)

                def down(j, i, slot):
                    b = R * j + i
                    pe.wait_ge(h_copied, b + 1)
                    wait(pe, y_copied, b - 1)
                    for c in range(FC):
                        last = nc.tensor.matmul(ps_y[i % 2][:, :], hT[i % 2][:, c * P:(c + 1) * P], slot_columns(slot, UP + c * C, C),
                                                start=c == 0, stop=c == FC - 1)
                    last.then_inc(down_done, 1)

                def first():
                    turn_x(0, 0)
                    up(0, 0, expert_of(0), weights(0))
                    turn_x(0, 1)

                def step(j, s):
                    b = R * j + s
                    expert, slot, slot_before = expert_of(b), weights(b), weights(b - 1)
                    turn_h(j, s - 1)
                    up(j, s, expert, slot)
                    turn_x(j, s + 1)
                    down(j, s - 1, slot_before)

                def last(j):
                    b = R * j + R - 1
                    expert, slot, slot_before = expert_of(b), weights(b), weights(b - 1)
                    turn_h(j, R - 2)
                    up(j, R - 1, expert, slot)
                    down(j, R - 2, slot_before)
                    turn_h(j, R - 1)
                    down(j, R - 1, slot)

                pe.sem_inc(down_done, 1)
                pipeline(pe, R, TURNS, first, step, last, last_turn=last_used(pe))

            @block.scalar
            def _(act):
                def copy_h(j, i):
                    act.wait_ge(h_turned, R * j + i + 1)
                    nc.scalar.activation(hT[i % 2][:, :], ps_h[i % 2][:, 0:F], ACT.Copy).then_inc(h_copied, 1)

                def silu(j, s):
                    act.wait_ge(up_done, R * j + s + 1)
                    wait(act, h_done, R * j + s - 1)
                    nc.scalar.activation(sg[s % 2][:, :], ps_u[s % 2][:, 0:F], ACT.Silu).then_inc(silu_done, 1)

                def copy_y(j, i):
                    b = R * j + i
                    act.wait_ge(down_done, b + 2)
                    uses = j + i // R
                    wait(act, y_out[i % R], 16 * uses)
                    nc.scalar.activation(y[i % R][:, :], ps_y[i % 2][:, :], ACT.Copy).then_inc(y_copied, 1)
                    act.wait_ge(y_copied, b + 1)
                    act.dma_start(rows_d[bass.ds(b * P, P), :], y[i % R][:, :]).then_inc(y_out[i % R], 16)

                def first():
                    silu(0, 0)

                def step(j, s):
                    copy_h(j, s - 1)
                    silu(j, s)
                    copy_y(j, s - 1)

                def last(j):
                    step(j, R - 1)
                    copy_h(j, R - 1)
                    copy_y(j, R - 1)

                last_turn = last_used(act)
                pipeline(act, R, TURNS, first, step, last, last_turn=last_turn)
                for s in range(R):
                    act.wait_ge(y_out[s], 16 * last_turn + 16)
                settled(act, passed_act)

            @block.vector
            def _(dve):
                def copy_x(j, i):
                    dve.wait_ge(x_turned, R * j + i + 1)
                    nc.vector.tensor_copy(xT[i % 2][:, :], ps_x[i % 2][:, :]).then_inc(x_copied, 1)

                def gated(j, s):
                    dve.wait_ge(silu_done, R * j + s + 1)
                    nc.vector.tensor_tensor(h[s % 2][:, :], sg[s % 2][:, :], ps_u[s % 2][:, F:2 * F], ALU.mult).then_inc(h_done, 1)

                def first():
                    copy_x(0, 0)
                    gated(0, 0)
                    copy_x(0, 1)

                def step(j, s):
                    gated(j, s)
                    copy_x(j, s + 1)

                def last(j):
                    gated(j, R - 1)

                nc.vector.memset(zero[:, :], 0.0).then_inc(zero_set, 1)
                pipeline(dve, R, TURNS, first, step, last, last_turn=last_used(dve))


def shared_and_combine(nc, up, down, tn_d, x1_d, rows_d, out, k_sb, gates, experts_of, slots_of, starts):
    tn_v, x1_v, out_v = (a.rearrange("(t p) c -> t p c", p=P) for a in (tn_d, x1_d, out))
    one_tile = lambda a, t: a[bass.ds(t, 1), :, :].rearrange("a p n -> (a p) n")
    PAIRS = NT // 2
    with ExitStack() as ctx:
        sb = lambda n, s, d=fp32: ctx.enter_context(nc.sbuf_tensor(n, s, d))
        sem = lambda n: ctx.enter_context(nc.semaphore("e_" + n))
        ps = lambda n: ctx.enter_context(nc.psum_tensor(n, [P, CH], fp32))
        tn = [sb(f"tn_{s}", [P, C]) for s in range(2)]
        x1 = [sb(f"x1_{s}", [P, C]) for s in range(2)]
        got = [[sb(f"got{s}{c}", [P, C]) for c in range(TOPK)] for s in range(2)]
        place = [sb(f"place{s}", [P, TOPK], i32) for s in range(2)]
        gate = [sb(f"gate{s}", [P, TOPK]) for s in range(2)]
        chosen, slot, row, spare_row = sb("chosen_", [P, TOPK, E]), sb("slot_", [P, TOPK]), sb("row_", [P, TOPK]), sb("spare_row", [P, 1])
        tnT, sg, h, hT, o = [[sb(f"{n}{s}", [P, C]) for s in range(2)] for n in ("tnT_", "sg_", "h_", "hT_", "o")]
        ps_x, ps_h = ps("ps_x_"), ps("ps_h_")
        ps_g, ps_u, ps_y = [[ps(f"{n}{s}") for s in range(2)] for n in ("ps_g_", "ps_u_", "ps_y_")]
        tn_in, x1_in, rows_in, stored = [[sem(f"{n}{s}") for s in range(2)] for n in ("tn_in", "x1_in", "rows_in", "stored")]
        setup, placed, tn_turned, tn_copied, up_done, silu_done, h_done, h_turned, h_copied, down_done, shared_in, dve_steps, done = [
            sem(n) for n in ("setup", "placed", "tn_turned", "tn_copied", "up_done", "silu_done", "h_done", "h_turned", "h_copied",
                             "down_done", "shared_in", "dve_steps", "done")]
        passed = sem("passed")

        with nc.Block() as block:
            @block.sync
            def _(sp):
                def turn(j):
                    for s in range(2):
                        wait(sp, tn_turned, 2 * j + s - 1)
                        sp.dma_start(tn[s][:, :], one_tile(tn_v, 2 * j + s)).then_inc(tn_in[s], 16)
                        wait(sp, shared_in, 2 * j + s - 1)
                        sp.dma_start(x1[s][:, :], one_tile(x1_v, 2 * j + s)).then_inc(x1_in[s], 16)

                turns(sp, PAIRS, turn)

            @block.gpsimd
            def _(pool):
                def turn(j):
                    for s in range(2):
                        pool.wait_ge(placed, 2 * j + s + 1)
                        settled(pool, passed)
                        for c in range(TOPK):
                            nc.gpsimd.indirect_dma_start(out=got[s][c][:, :], out_offset=None, in_=rows_d,
                                                         in_offset=bass.IndirectOffsetOnAxis(place[s][:, c:c + 1], 0)).then_inc(rows_in[s], 16)

                turns(pool, PAIRS, turn)

            @block.tensor
            def _(pe):
                ident = k_sb[:, K_ID:K_ID + P]

                def turn_tokens(j, i):
                    t = 2 * j + i
                    pe.wait_ge(tn_in[i % 2], 16 * (j + i // 2 + 1))
                    wait(pe, tn_copied, t)
                    for c in range(CC):
                        at = slice(c * P, (c + 1) * P)
                        last = nc.tensor.transpose(ps_x[:, at], tn[i % 2][:, at], ident)
                    last.then_inc(tn_turned, 1)

                def go_up(j, s):
                    t = 2 * j + s
                    pe.wait_ge(tn_copied, t + 1)
                    wait(pe, h_done, t - 1)
                    for bank, at in ((ps_g[s], 0), (ps_u[s], SH)):
                        for c in range(CC):
                            last = nc.tensor.matmul(bank[:, :], tnT[s][:, c * P:(c + 1) * P], up[:, c, at:at + SH], start=c == 0, stop=c == CC - 1)
                        last.then_inc(up_done, 1)

                def turn_hidden(j, i):
                    t = 2 * j + i
                    pe.wait_ge(h_done, t + 1)
                    wait(pe, h_copied, t)
                    for c in range(SC):
                        at = slice(c * P, (c + 1) * P)
                        last = nc.tensor.transpose(ps_h[:, at], h[i % 2][:, at], ident)
                    last.then_inc(h_turned, 1)

                def go_down(j, i):
                    t = 2 * j + i
                    pe.wait_ge(h_copied, t + 1)
                    wait(pe, shared_in, t - 1)
                    for c in range(SC):
                        last = nc.tensor.matmul(ps_y[i % 2][:, :], hT[i % 2][:, c * P:(c + 1) * P], down[:, c, :], start=c == 0, stop=c == SC - 1)
                    last.then_inc(down_done, 1)

                def first():
                    turn_tokens(0, 0)
                    go_up(0, 0)
                    turn_tokens(0, 1)

                def step(j, s):
                    turn_hidden(j, s - 1)
                    go_up(j, s)
                    turn_tokens(j, s + 1)
                    go_down(j, s - 1)

                def last(j):
                    turn_hidden(j, 0)
                    go_up(j, 1)
                    go_down(j, 0)
                    turn_hidden(j, 1)
                    go_down(j, 1)

                pipeline(pe, 2, PAIRS, first, step, last)

            @block.scalar
            def _(act):
                def copy_tokens(j, i):
                    t = 2 * j + i
                    act.wait_ge(tn_turned, t + 1)
                    wait(act, up_done, 2 * t - 2)
                    nc.scalar.activation(tnT[i % 2][:, :], ps_x[:, :], ACT.Copy).then_inc(tn_copied, 1)

                def silu(j, s):
                    t = 2 * j + s
                    act.wait_ge(up_done, 2 * t + 1)
                    wait(act, h_done, t - 1)
                    nc.scalar.activation(sg[s][:, :], ps_g[s][:, :], ACT.Silu).then_inc(silu_done, 1)

                def copy_hidden(j, i):
                    t = 2 * j + i
                    act.wait_ge(h_turned, t + 1)
                    wait(act, down_done, t - 1)
                    nc.scalar.activation(hT[i % 2][:, :], ps_h[:, :], ACT.Copy).then_inc(h_copied, 1)

                def store(j, i):
                    act.wait_ge(done, 2 * j + i + 1)
                    act.dma_start(one_tile(out_v, 2 * j + i), o[i % 2][:, :]).then_inc(stored[i % 2], 16)

                def first():
                    copy_tokens(0, 0)
                    silu(0, 0)
                    copy_tokens(0, 1)

                def step(j, s):
                    copy_hidden(j, s - 1)
                    silu(j, s)
                    copy_tokens(j, s + 1)
                    if not (isinstance(j, int) and j == 0):
                        store(j, s - 2)

                def last(j):
                    copy_hidden(j, 0)
                    silu(j, 1)
                    store(j, -1)
                    copy_hidden(j, 1)
                    store(j, 0)
                    store(j, 1)

                pipeline(act, 2, PAIRS, first, step, last)
                for s in range(2):
                    act.wait_ge(stored[s], 16 * PAIRS)

            @block.vector
            def _(dve):
                link = Chain(dve, dve_steps)
                nc.vector.tensor_scalar(spare_row[:, :], k_sb[:, K_P:K_P + 1], float((NB - 1) * P), None, ALU.add).then_inc(setup, 1)
                dve.wait_ge(setup, 1)

                def place_rows(j, i):
                    t, s = 2 * j + i, i % 2
                    at = bass.ds(t * TOPK, TOPK)
                    nc.vector.tensor_copy(gate[s][:, :], gates[:, at])
                    link(nc.vector.tensor_copy(slot[:, :], slots_of[:, at]))
                    link(nc.vector.tensor_tensor(chosen[:, :, :], k_sb[:, K_IOTA:K_IOTA + E].unsqueeze(1).to_broadcast([P, TOPK, E]),
                                                 experts_of[:, at].unsqueeze(2).to_broadcast([P, TOPK, E]), ALU.is_equal))
                    link(nc.vector.tensor_tensor(chosen[:, :, :], chosen[:, :, :], starts[:, :].unsqueeze(1).to_broadcast([P, TOPK, E]), ALU.mult))
                    link(nc.vector.tensor_reduce(row[:, :], chosen[:, :, :], AX.X, ALU.add))
                    link(nc.vector.tensor_tensor(row[:, :], row[:, :], slot[:, :], ALU.add))
                    link(nc.vector.tensor_scalar(slot[:, :], slot[:, :], float(CAP), None, ALU.is_lt))
                    link(nc.vector.scalar_tensor_tensor(row[:, :], row[:, :], spare_row[:, :], slot[:, :], ALU.subtract, ALU.mult))
                    nc.vector.tensor_scalar(place[s][:, :], row[:, :], spare_row[:, :], None, ALU.add).then_inc(placed, 1)
                    dve.wait_ge(placed, t + 1)

                def gated(j, s):
                    t = 2 * j + s
                    dve.wait_ge(silu_done, t + 1)
                    dve.wait_ge(up_done, 2 * t + 2)
                    wait(dve, h_turned, t - 1)
                    nc.vector.tensor_tensor(h[s][:, :], sg[s][:, :], ps_u[s][:, :], ALU.mult).then_inc(h_done, 1)

                def combine(j, i):
                    t, s, turn = 2 * j + i, i % 2, j + i // 2
                    dve.wait_ge(down_done, t + 1)
                    dve.wait_ge(x1_in[s], 16 * turn + 16)
                    wait(dve, stored[s], 16 * turn)
                    nc.vector.scalar_tensor_tensor(o[s][:, :], ps_y[s][:, :], 0.5, x1[s][:, :], ALU.mult, ALU.add).then_inc(shared_in, 1)
                    dve.wait_ge(shared_in, t + 1)
                    dve.wait_ge(rows_in[s], 16 * TOPK * (turn + 1))
                    for c in range(TOPK):
                        add = nc.vector.scalar_tensor_tensor(o[s][:, :], got[s][c][:, :], gate[s][:, c:c + 1], o[s][:, :], ALU.mult, ALU.add)
                        if c < TOPK - 1:
                            link(add)
                    add.then_inc(done, 1)
                    dve.wait_ge(done, t + 1)

                def first():
                    place_rows(0, 0)
                    gated(0, 0)
                    place_rows(0, 1)

                def step(j, s):
                    gated(j, s)
                    combine(j, s - 1)
                    place_rows(j, s + 1)

                def last(j):
                    gated(j, 1)
                    combine(j, 0)
                    combine(j, 1)

                pipeline(dve, 2, PAIRS, first, step, last, link, 2 * (TOPK - 1 + 7))


def program(nc, x, x_tok, pos, freq, w_qkv, taps, w_out, b_out, router_w, router_b, sh_up, sh_down, experts, masks, consts, out):
    dram = lambda n, s, d=fp32: nc.dram_tensor(n, s, d, kind="Internal").ap()
    cos_d, sin_d = dram("cos_d", [P, N]), dram("sin_d", [P, N])
    qk_d = dram("qk_d", [2 * CC, P, N])
    v_d = dram("v_d", [N, C])
    x1_d, tn_d = dram("x1_d", [N, C]), dram("tn_d", [N, C])
    ids_d = dram("ids_d", [SLOTS, 1], i32)
    rows_d = dram("rows_d", [NB * P, C])
    with ExitStack() as ctx:
        sb = lambda n, s, d=fp32: ctx.enter_context(nc.sbuf_tensor(n, s, d))
        k_sb = sb("k_sb", [P, K_END])
        k_in = ctx.enter_context(nc.semaphore("k_in"))
        with nc.Block() as block:
            @block.sync
            def _(sp):
                sp.dma_start(k_sb[:, :], consts).then_inc(k_in, 16)
                sp.wait_ge(k_in, 16)
        with nc.sbuf_tensor("xn", [P, CC, N], fp32) as xn:
            layernorm_and_tables(nc, x, pos, freq, cos_d, sin_d, xn)
            qkv_conv_rotary(nc, w_qkv, taps, cos_d, sin_d, qk_d, v_d, xn, k_sb)
        gates, experts_of, slots_of = [sb(n, [P, NT * TOPK]) for n in ("gates", "experts_of", "slots_of")]
        starts = sb("starts", [P, E])
        blocks = Blocks(sb)
        attention_and_routing(nc, x_tok, masks, w_out, b_out, router_w, router_b, qk_d, v_d, x1_d, tn_d, ids_d,
                              k_sb, gates, experts_of, slots_of, starts, blocks)
        up, down = sb("up", [P, CC, 2 * SH]), sb("down", [P, SC, C])
        expert_blocks(nc, experts, tn_d, ids_d, rows_d, k_sb, blocks, ((up, sh_up), (down, sh_down)))
        shared_and_combine(nc, up, down, tn_d, x1_d, rows_d, out, k_sb, gates, experts_of, slots_of, starts)


def shape_constants():
    import numpy as np
    k = np.zeros((P, K_END), np.float32)
    i = np.arange(P)
    k[:, K_ID:K_ID + P] = i[:, None] == i[None, :]
    k[:, K_BEFORE:K_BEFORE + P] = i[:, None] < i[None, :]
    k[:E, K_UPTO:K_UPTO + E] = i[:E, None] <= i[None, :E]
    k[:, K_IOTA:K_IOTA + NB] = np.arange(NB)
    k[:, K_P] = i
    for h in range(P // HD):
        for r in range(RH):
            a = h * HD + r
            k[a + RH, K_ROT + a] = -1.0
            k[a, K_ROT + a + RH] = 1.0
    row, col = i // IMG, i % IMG
    first_col = np.clip(col - KW // 2, 0, IMG - KW)
    key_row, key_col = np.arange(WIN) // IMG, np.arange(WIN) % IMG
    in_cols = (key_col[None] >= first_col[:, None]) & (key_col[None] < first_col[:, None] + KW)
    masks = []
    for first_row in (0 * row, row, 0 * row + 1):
        in_rows = (key_row[None] >= first_row[:, None]) & (key_row[None] < first_row[:, None] + KW)
        masks.append(np.where(in_rows & in_cols, 0.0, -1e30))
    return k, np.stack(masks).astype(np.float32)


def layout(x, L0_conv_pos, L0_conv_w_qkv, L0_conv_w_dw, L0_conv_b_dw, L0_conv_freqs, L0_conv_w_out, L0_conv_b_out,
           L0_ffn_router_w, L0_ffn_bias, L0_ffn_shared_w_gate, L0_ffn_shared_w_up, L0_ffn_shared_w_down,
           L0_ffn_w_gate, L0_ffn_w_up, L0_ffn_w_down):
    import numpy as np
    k, masks = shape_constants()
    img = np.asarray(x).reshape(C, N)
    pos = np.asarray(L0_conv_pos).reshape(N, 2).T
    pos = np.broadcast_to(pos[None, :, None, :], (NH, 2, RH // 2, N)).reshape(P, N)
    freq = np.broadcast_to(np.asarray(L0_conv_freqs)[:, None, :], (NH, 2, RH // 2)).reshape(P, 1)
    order = [o for h in range(CC) for o in (h, CC + h)] + [2 * CC + h for h in range(CC)]
    w_qkv = np.asarray(L0_conv_w_qkv).reshape(3 * CC, P, CC, P)[order].transpose(0, 3, 2, 1)
    taps = np.concatenate([np.asarray(L0_conv_w_dw).reshape(3 * CC, P, TAPS), np.asarray(L0_conv_b_dw).reshape(3 * CC, P, 1)], 2)[order]
    chunks = lambda w: w.reshape(-1, P, w.shape[-1]).transpose(1, 0, 2)
    w_out = chunks(np.asarray(L0_conv_w_out).T)
    router = chunks(np.asarray(L0_ffn_router_w).T)
    gate, up = (np.asarray(w).reshape(2 * F, C).T for w in (L0_ffn_shared_w_gate, L0_ffn_shared_w_up))
    sh_up = np.concatenate([chunks(gate), chunks(up)], 2)
    sh_down = chunks(np.asarray(L0_ffn_shared_w_down).transpose(0, 2, 1).reshape(2 * F, C))
    wg, wu = (np.asarray(w).transpose(0, 2, 1).reshape(E, CC, P, F) for w in (L0_ffn_w_gate, L0_ffn_w_up))
    up_both = np.concatenate([wg, wu], 3).transpose(0, 2, 1, 3).reshape(E, P, CC * 2 * F)
    down = np.asarray(L0_ffn_w_down).transpose(0, 2, 1).reshape(E, FC, P, C).transpose(0, 2, 1, 3).reshape(E, P, FC * C)
    return {
        "x": img, "x_tok": img.T, "pos": pos, "freq": freq, "w_qkv": w_qkv, "taps": taps, "w_out": w_out,
        "b_out": np.asarray(L0_conv_b_out).reshape(1, C), "router_w": router,
        "router_b": np.asarray(L0_ffn_bias).reshape(1, E), "sh_up": sh_up, "sh_down": sh_down,
        "experts": np.concatenate([up_both, down], 2), "masks": masks, "consts": k,
    }


def kernel(**inputs):
    import numpy as np
    import concourse.bacc as bacc
    from concourse.bass_utils import run_bass_kernel_spmd

    arrays = {n: np.ascontiguousarray(a) for n, a in layout(**inputs).items()}
    nc = bacc.Bacc("TRN2", target_bir_lowering=False, num_devices=1)
    args = {n: nc.dram_tensor("in_" + n, a.shape, mybir.dt.from_np(a.dtype), kind="ExternalInput").ap() for n, a in arrays.items()}
    out = nc.dram_tensor("out_tok", [N, C], fp32, kind="ExternalOutput").ap()
    program(nc, out=out, **args)
    r = run_bass_kernel_spmd(nc, [{"in_" + n: a for n, a in arrays.items()}], core_ids=[0])
    return np.ascontiguousarray(r.results[0]["out_tok"].T).reshape(1, C, IMG, IMG)
```
